# Optimizing a Trainium2 kernel written in Bass

```python
import numpy as np
import jax
import jax.numpy as jnp

def _softmax(x, axis=-1):
    return jax.nn.softmax(x, axis=axis)

def _gelu(x):
    return jax.nn.gelu(x, approximate=True)

def _silu(x):
    return jax.nn.silu(x)

def _sigmoid(x):
    return jax.nn.sigmoid(x)

def _layernorm(x, axis=-1, eps=1e-05):
    m = jnp.mean(x, axis=axis, keepdims=True)
    v = jnp.var(x, axis=axis, keepdims=True)
    return (x - m) / jnp.sqrt(v + eps)

def _scatter_add(tgt, idx, src, axis=0):
    return tgt.at[idx].add(src)

def _segment_sum(src, seg, n):
    return jax.ops.segment_sum(src, seg, n)
kernel_name = 'mk_vit_tower_cls_d1_tok_img4096_r4_cd5f4c'

def setup_inputs(seed: int=0):
    np.random.seed(seed)
    _w = jnp.asarray

    def _rec_inputs():
        import jax
        import jax.numpy as jnp
        _rk = jax.random.key(seed)
        x = -0.0043416 + 0.998921 * jax.random.normal(jax.random.fold_in(_rk, 1), (32, 64, 64, 2), jnp.float32)
        cls_tok = 0.02 * jax.random.normal(jax.random.fold_in(_rk, 5), (1, 1, 1024), jnp.float32)
        return (x, cls_tok)
    x, cls_tok = _rec_inputs()

    def _L0_tok_setup():
        import jax, jax.numpy as jnp
        import numpy as np
        H, N, CH = (64, 64, 1)
        key = jax.random.key(seed)
        k1, k2, k3 = jax.random.split(key, 3)
        A_abslog = jnp.log(jax.random.uniform(k1, (H, N), dtype=jnp.float32, minval=0.5, maxval=0.999))
        A_phase = jax.random.uniform(k2, (H, N), dtype=jnp.float32, minval=-np.pi, maxval=np.pi)
        C = jax.random.normal(k3, (CH, H, N, 2), dtype=jnp.float32)
        return {'A_abslog': A_abslog, 'A_phase': A_phase, 'C': C, 'L': 1024}
    _L0_tok_all = _L0_tok_setup()
    _L0_tok_in = {k: v for k, v in _L0_tok_all.items() if k in ('A_abslog', 'A_phase')}
    del _L0_tok_all

    def _L0_attn_setup():
        import jax, jax.numpy as jnp
        import numpy as np
        EMB = 1024
        HEADS = 32
        SCALE = 4
        D = EMB // HEADS
        HKV = HEADS // SCALE
        B, S = (2, 512)
        key = jax.random.key(seed)
        ks = jax.random.split(key, 7)
        std = 0.02
        return {'x': jax.random.normal(ks[0], (B, S, EMB), jnp.float32), 'Wq': jax.random.normal(ks[1], (EMB, D, HEADS), jnp.float32) * std, 'bq': jnp.zeros((D, HEADS), jnp.float32), 'Wk': jax.random.normal(ks[2], (EMB, D, HKV), jnp.float32) * std, 'bk': jnp.zeros((D, HKV), jnp.float32), 'Wv': jax.random.normal(ks[3], (EMB, D, HKV), jnp.float32) * std, 'bv': jnp.zeros((D, HKV), jnp.float32)}
    _L0_attn_all = _L0_attn_setup()
    _L0_attn_in = {k: v for k, v in _L0_attn_all.items() if k in ('Wq', 'bq', 'Wk', 'bk', 'Wv', 'bv')}
    del _L0_attn_all

    def _L0_ffn_setup():
        import jax, jax.numpy as jnp
        import numpy as np
        key = jax.random.key(seed)
        k = jax.random.split(key, 6)
        x = jax.random.normal(k[0], (4, 512, 1024), jnp.float32)
        W = jax.random.normal(k[1], (1024, 1024), jnp.float32) * 0.02
        bias = jax.random.normal(k[2], (1024,), jnp.float32) * 0.02
        A = jax.random.normal(k[3], (16, 16, 1024), jnp.float32) * 0.02
        Bf = jax.random.normal(k[4], (16, 1024, 16), jnp.float32) * 0.02
        coeffs = jax.random.uniform(k[5], (16,), jnp.float32)
        scales = jnp.full((16,), 0.5, jnp.float32)
        return {'x': x, 'W': W, 'bias': bias, 'A': A, 'Bf': Bf, 'coeffs': coeffs, 'scales': scales}
    _L0_ffn_all = _L0_ffn_setup()
    _L0_ffn_in = {k: v for k, v in _L0_ffn_all.items() if k in ('W', 'bias', 'A', 'Bf', 'coeffs', 'scales')}
    del _L0_ffn_all
    return {'x': x, 'cls_tok': cls_tok, 'L0_tok_A_abslog': _L0_tok_in['A_abslog'], 'L0_tok_A_phase': _L0_tok_in['A_phase'], 'L0_attn_Wq': _L0_attn_in['Wq'], 'L0_attn_bq': _L0_attn_in['bq'], 'L0_attn_Wk': _L0_attn_in['Wk'], 'L0_attn_bk': _L0_attn_in['bk'], 'L0_attn_Wv': _L0_attn_in['Wv'], 'L0_attn_bv': _L0_attn_in['bv'], 'L0_ffn_W': _L0_ffn_in['W'], 'L0_ffn_bias': _L0_ffn_in['bias'], 'L0_ffn_A': _L0_ffn_in['A'], 'L0_ffn_Bf': _L0_ffn_in['Bf'], 'L0_ffn_coeffs': _L0_ffn_in['coeffs'], 'L0_ffn_scales': _L0_ffn_in['scales']}

def reference(x, cls_tok, L0_tok_A_abslog, L0_tok_A_phase, L0_attn_Wq, L0_attn_bq, L0_attn_Wk, L0_attn_bk, L0_attn_Wv, L0_attn_bv, L0_ffn_W, L0_ffn_bias, L0_ffn_A, L0_ffn_Bf, L0_ffn_coeffs, L0_ffn_scales):
    import jax
    import jax.numpy as jnp

    def _L0_tok_ref(A_abslog, A_phase, C, L):
        import jax, jax.numpy as jnp
        import numpy as np
        H, N, CH = (64, 64, 1)
        A = jnp.exp(A_abslog + 1j * A_phase)
        dtA = jnp.log(A)
        Cc = C[..., 0] + 1j * C[..., 1]
        Cc = Cc * (A - 1.0) / dtA
        t = jnp.arange(L, dtype=jnp.float32)
        K = jnp.exp(dtA[:, :, None] * t)
        K = jnp.einsum('chn,hnl->chl', Cc, K)
        return 2.0 * K.real

    def _L0_attn_ref(x, Wq, bq, Wk, bk, Wv, bv):
        import jax, jax.numpy as jnp
        import numpy as np
        EMB = 1024
        HEADS = 32
        SCALE = 4
        D = EMB // HEADS
        HKV = HEADS // SCALE
        B, S = (2, 512)
        q = jnp.einsum('bse,edh->bsdh', x, Wq) + bq
        k = jnp.einsum('bse,edh->bsdh', x, Wk) + bk
        v = jnp.einsum('bse,edh->bsdh', x, Wv) + bv
        k = jnp.repeat(k, SCALE, axis=-1)
        v = jnp.repeat(v, SCALE, axis=-1)
        scores = jnp.einsum('bsdh,bseh->bsde', q, k) / np.float32(np.sqrt(D))
        attn = jax.nn.softmax(scores, axis=-1)
        out = jnp.einsum('bsde,bseh->bsdh', attn, v)
        return out.reshape(x.shape[:-1] + (EMB,))

    def _L0_ffn_ref(x, W, bias, A, Bf, coeffs, scales):
        import jax, jax.numpy as jnp
        import numpy as np
        out = jnp.einsum('bsd,od->bso', x, W) + bias
        xa = jnp.einsum('bsd,erd->ebsr', x, A)
        w = coeffs * scales
        upd = jnp.einsum('ebsr,eor,e->bso', xa, Bf, w)
        return out + upd
    h = _L0_tok_ref(L0_tok_A_abslog, L0_tok_A_phase, x, 1024)
    h = jnp.concatenate([jnp.broadcast_to(cls_tok, (h.shape[0], 1, h.shape[2])), h], axis=1)
    h = h + _L0_attn_ref(_layernorm(h, axis=-1), L0_attn_Wq, L0_attn_bq, L0_attn_Wk, L0_attn_bk, L0_attn_Wv, L0_attn_bv)
    h = h + _L0_ffn_ref(_layernorm(h, axis=-1), L0_ffn_W, L0_ffn_bias, L0_ffn_A, L0_ffn_Bf, L0_ffn_coeffs, L0_ffn_scales)
    return h

_drawn_inputs = setup_inputs


def setup_inputs(seed=0):
    import zlib

    import numpy as np

    out = dict(_drawn_inputs(seed))
    spreads = {'L0_attn_bq': (0.0, 0.8),
     'L0_attn_bk': (0.0, 0.8),
     'L0_attn_bv': (0.0, 0.418),
     'L0_ffn_scales': (0.5, 0.6)}
    factors = {'L0_ffn_bias': 3.537, 'L0_ffn_coeffs': 2.813}
    for name, (base, spread) in spreads.items():
        noise = np.random.default_rng([zlib.crc32(name.encode()), seed]).standard_normal(out[name].shape)
        drawn = base * np.exp(spread * noise) if base else spread * noise
        out[name] = jnp.asarray(drawn.astype(out[name].dtype))
    for name, factor in factors.items():
        out[name] = (out[name] * factor).astype(out[name].dtype)
    return out
```

```python
from contextlib import ExitStack

import concourse.bass as bass
import numpy as np
from concourse import mybir

ALU = mybir.AluOpType
ACT = mybir.ActivationFunctionType
AX_X = mybir.AxisListType.X
F32 = mybir.dt.float32
F32R = mybir.dt.float32r

P = 128
C, H, N, L = 32, 64, 64, 1024
K = L // P
R, S, B = 4, 4, 8
D, G, J = 32, 8, 4
QK = 2 * G * D
QKV = 3 * G * D
ER = 256
GROUPS = 1 + H // R
GV = G + 1
EPS = 1e-5

T_B1, T_B2, T_AR, T_AI, T_V1, T_V2, T_ONE = 0, 16, 32, 40, 48, 56, 64
T_ALL = 66
T_KEPT = T_V1
HC = 8

C_ID, C_PERM, C_MR, C_MS, C_POW, C_OFF = 0, 128, 256, 260, 264, 264 + T_ALL
C_ALL = C_OFF + T_ALL
ROUND = 1.5 * 2.0 ** 23
INV_HI = float(np.floor(2.0 ** 14 / (2 * np.pi)) / 2.0 ** 14)
INV_LO = float(1 / (2 * np.pi) - INV_HI)
TWO_PI = 6.283185


def constants():
    c = np.zeros((P, C_ALL), np.float32)
    p = np.arange(P)
    c[p, C_ID + p] = 1
    r, b, s = p // 32, p % 32 // 4, p % 4
    c[32 * s + 4 * b + r, C_PERM + p] = 1
    c[p, C_MR + p // 32] = 1
    c[p, C_MS + p % 32 // 8] = 1
    top = p < N
    power, off = np.zeros(T_ALL), np.zeros((2, T_ALL))
    for at, n, m, hi, lo in [(T_B1, 16, 8, 0.25, 0.0), (T_B2, 16, 8, 0.5, 0.25),
                             (T_AR, 8, 128, 0.25, 0.25), (T_AI, 8, 128, 0.0, 0.0),
                             (T_V1, 8, 1, 0.25, 0.5), (T_V2, 8, 1, 0.5, 0.75)]:
        power[at:at + n] = m * np.arange(n)
        off[0, at:at + n], off[1, at:at + n] = hi, lo
    power[T_ONE:] = 1
    off[:, T_ONE] = 0.25
    c[:, C_POW:C_POW + T_ALL] = power
    c[:, C_OFF:C_OFF + T_ALL] = np.where(top[:, None], off[0], off[1])
    return c


class Chain:

    def __init__(self, eng, sem):
        self.eng, self.sem, self.n, self.past = eng, sem, 0, 0

    def __call__(self, ins):
        self.n += 1
        ins.then_inc(self.sem, 1)
        self.eng.wait_ge(self.sem, self.past + self.n)

    def enter(self, i, per_pass):
        self.past, self.at, self.per_pass = i * per_pass, self.n, per_pass

    def leave(self, passes):
        assert self.n - self.at == self.per_pass, (self.n - self.at, self.per_pass)
        self.n, self.past = self.at + passes * self.per_pass, 0


def tower(nc, x, alog, phase, cls, wq, wkv, bq, bkv, wt, fbias, fa, fb, gates, const, out):
    ctx = ExitStack()
    with ctx:
        sem = lambda name: ctx.enter_context(nc.semaphore(name))

        def sb(name, shape, dt=F32, into=ctx):
            return into.enter_context(nc.sbuf_tensor(name, shape, dt))

        wh, wl = sb("wh", [P, K, QKV], F32R), sb("wl", [P, K, QKV], F32R)
        fh, fl = sb("fh", [P, K, L], F32R), sb("fl", [P, K, L], F32R)
        tab = sb("tab", [P, H, T_KEPT])
        u1, u2 = sb("u1", [P, H, 8]), sb("u2", [P, H, 8])
        cst = sb("cst", [P, C_ALL])
        identr = sb("identr", [P, P], F32R)
        qkv_bias, ffn_bias = sb("qkv_bias", [P, QKV]), sb("ffn_bias", [P, L])
        clst = sb("clst", [P, K])
        stat = sb("stat", [P, 16])
        half = sb("half", [P, 1])
        perm = cst[:, C_PERM:C_PERM + P]
        mask_r = cst[:, C_MR:C_MR + R]
        mask_s = cst[:, C_MS:C_MS + S]

        T = ctx.enter_context(nc.psum_tensor("T", [P, L], F32))
        Q = ctx.enter_context(nc.psum_tensor("Q", [P, L], F32))
        HT = ctx.enter_context(nc.psum_tensor("HT", [P, L], F32))
        F = ctx.enter_context(nc.psum_tensor("F", [P, L], F32))
        O = F[:, 0:B * R * GV].rearrange("p (b r g) -> p b r g", b=B, r=R)
        OT = HT[:, 512:768].rearrange("p (q n) -> p q n", q=2)
        OTOK = HT[:, 0:256]

        scratch = [nc.dram_tensor(f"qk_scratch{i}", (2, P, G * D), F32, kind="Internal").ap()
                   for i in range(2)]

        with ExitStack() as early:
            ph, al = sb("ph", [P, H], F32, early), sb("al", [P, H], F32, early)
            small = sb("small", [P, 14, H], F32, early)
            phr = sb("phr", [P, 2, H], F32R, early)
            arg = sb("arg", [P, HC, T_ALL], F32, early)
            turns = sb("turns", [P, HC, T_ALL], F32, early)
            mag = sb("mag", [P, HC, T_ALL], F32, early)
            vone = sb("vone", [P, H, T_ALL - T_KEPT], F32, early)
            stage = sb("stage", [P, K, L], F32, early)
            lora_a, lora_b = sb("lora_a", [P, 2, L], F32, early), sb("lora_b", [P, 2, L], F32, early)
            gate = sb("gate", [P, 4], F32, early)
            bq_raw = sb("bq_raw", [P, L], F32, early)
            ones = sb("ones", [P, P], F32, early)
            flat = stage[:, :, :].rearrange("p k n -> p (k n)")
            wsum = flat[:, 0:K * QKV].rearrange("p (k n) -> p k n", k=K)
            ring = flat[:, K * QKV:].rearrange("p (i n) -> p i n", i=2)

            small_in, wkv_in = sem("small_in"), sem("wkv_in")
            wq_in = [sem(f"wq_in{i}") for i in range(2)]
            lora_in, wt_in = sem("lora_in"), sem("wt_in")
            dve0, act0 = sem("dve_setup"), sem("act_setup")
            args_ready, mags_ready = sem("args_ready"), sem("mags_ready")
            sines_done, mags_done, table_done = sem("sines_done"), sem("mags_done"), sem("table_done")
            wq_summed, wsum_ready = sem("wq_summed"), sem("wsum_ready")
            mean_done, centred, w_hi_done = sem("mean_done"), sem("centred"), sem("w_hi_done")
            w_split, lora_scaled = sem("w_split"), sem("lora_scaled")
            lora_done, merged = sem("lora_done"), sem("merged")
            fmean_done, f_centred, f_hi_done = sem("fmean_done"), sem("f_centred"), sem("f_hi_done")
            banks = [T, Q, HT, F]

            with nc.Block() as block:
                @block.sync
                def _(sp):
                    for half_ in range(2):
                        sp.dma_start(ph[N * half_:N * half_ + N, :], phase).then_inc(small_in, 16)
                        sp.dma_start(al[N * half_:N * half_ + N, :], alog).then_inc(small_in, 16)
                    sp.dma_start(cst[:, :], const).then_inc(small_in, 16)
                    sp.dma_start(clst[:, :], cls.rearrange("(a k) -> a k", k=K)).then_inc(small_in, 16)
                    sp.dma_start(bq_raw[:, :], bq.partition_broadcast(P)).then_inc(small_in, 16)
                    sp.dma_start(qkv_bias[:, G * D:], bkv.partition_broadcast(P)).then_inc(small_in, 16)
                    sp.dma_start(ffn_bias[:, :], fbias.partition_broadcast(P)).then_inc(small_in, 16)
                    sp.dma_start(gate[:, :], gates).then_inc(small_in, 16)
                    sp.dma_start(wsum[:, :, G * D:], wkv.rearrange("(a k) n -> a k n", k=K)).then_inc(wkv_in, 16)
                    wq_v = wq.rearrange("(a k) n -> a k n", k=K)
                    for k in range(K):
                        if k >= 2:
                            sp.wait_ge(wq_summed, k - 1)
                        sp.dma_start(ring[:, k % 2, :], wq_v[:, k, :]).then_inc(wq_in[k % 2], 16)
                    sp.dma_start(lora_a[:, :, :], fa.rearrange("(q p) n -> p q n", p=P)).then_inc(lora_in, 16)
                    sp.dma_start(lora_b[:, :, :], fb.rearrange("(q p) n -> p q n", p=P)).then_inc(lora_in, 16)
                    sp.wait_ge(w_split, K)
                    sp.dma_start(stage[:, :, :], wt.rearrange("(a k) n -> a k n", k=K)).then_inc(wt_in, 16)

                @block.scalar
                def _(act):
                    for h in range(H // HC):
                        act.wait_ge(args_ready, h + 1)
                        nc.scalar.activation(arg[:, :, :], arg[:, :, :], ACT.Sin, scale=TWO_PI).then_inc(sines_done, 1)
                        act.wait_ge(mags_ready, h + 1)
                        nc.scalar.activation(mag[:, :, :], mag[:, :, :], ACT.Exp).then_inc(mags_done, 1)
                    for k in range(K):
                        act.wait_ge(centred, k + 1)
                        nc.scalar.activation(wh[:, k, :], wsum[:, k, :], ACT.Copy).then_inc(w_hi_done, 1)
                    for k in range(K):
                        act.wait_ge(f_centred, k + 1)
                        nc.scalar.activation(fh[:, k, :], stage[:, k, :], ACT.Copy).then_inc(f_hi_done, 1)

                @block.tensor
                def _(pe):
                    pe.wait_ge(wsum_ready, 1)
                    for h in range(2):
                        for k in range(K):
                            m = nc.tensor.matmul(Q[:, 512 * h:512 * h + 384], ones[:, :], wsum[:, k, 384 * h:384 * h + 384],
                                                 start=(k == 0), stop=(k == K - 1))
                    m.then_inc(mean_done, 1)
                    pe.wait_ge(lora_scaled, 1)
                    for k in range(K):
                        if k == 1:
                            pe.wait_ge(centred, K)
                        if k >= 4:
                            pe.wait_ge(merged, k - 3)
                        for o in range(2):
                            for q in range(2):
                                m = nc.tensor.matmul(banks[k % 4][:, 512 * o:512 * o + 512], lora_a[:, q, P * k:P * k + P],
                                                     lora_b[:, q, 512 * o:512 * o + 512], start=(q == 0), stop=(q == 1))
                        m.then_inc(lora_done, 1)
                    pe.wait_ge(merged, K)
                    for o in range(2):
                        for k in range(K):
                            m = nc.tensor.matmul(T[:, 512 * o:512 * o + 512], ones[:, :], stage[:, k, 512 * o:512 * o + 512],
                                                 start=(k == 0), stop=(k == K - 1))
                    m.then_inc(fmean_done, 1)

                @block.vector
                def _(dve):
                    v = nc.vector
                    link = Chain(dve, dve0)
                    tt = lambda o, a, b, op: link(v.tensor_tensor(o, a, b, op))
                    link(v.memset(ones[:, :], 1.0 / L))
                    link(v.memset(half[:, :], -0.5))
                    dve.wait_ge(small_in, 10 * 16)
                    link(v.tensor_copy(identr[:, :], cst[:, C_ID:C_ID + P]))
                    link(v.tensor_copy(phr[:, 0, :], ph[:, :]))
                    p_hi = phr[:, 0, :].bitcast(F32)
                    t_hi = phr[:, 1, :].bitcast(F32)
                    sm = lambda i: small[:, i, :]
                    tt(sm(0), ph[:, :], p_hi, ALU.subtract)
                    link(v.tensor_scalar(sm(1), p_hi, INV_HI, None, ALU.mult))
                    link(v.tensor_copy(phr[:, 1, :], sm(1)))
                    tt(sm(1), sm(1), t_hi, ALU.subtract)
                    link(v.scalar_tensor_tensor(sm(1), p_hi, INV_LO, sm(1), ALU.mult, ALU.add))
                    link(v.scalar_tensor_tensor(sm(1), sm(0), INV_HI + INV_LO, sm(1), ALU.mult, ALU.add))
                    link(v.tensor_scalar(sm(2), t_hi, ROUND, ROUND, ALU.add, ALU.subtract))
                    tt(sm(2), t_hi, sm(2), ALU.subtract)
                    tt(sm(2), sm(2), sm(1), ALU.add)
                    link(v.tensor_scalar(sm(3), sm(2), ROUND, ROUND, ALU.add, ALU.subtract))
                    tt(sm(2), sm(2), sm(3), ALU.subtract)
                    link(v.tensor_scalar(sm(2), sm(2), float(2 * np.pi), None, ALU.mult))

                    power = cst[:, C_POW:C_POW + T_ALL].unsqueeze(1).to_broadcast([P, HC, T_ALL])
                    off = cst[:, C_OFF:C_OFF + T_ALL].unsqueeze(1).to_broadcast([P, HC, T_ALL])
                    for h in range(H // HC):
                        hs = slice(HC * h, HC * h + HC)
                        wide = lambda a: a[:, hs].unsqueeze(2).to_broadcast([P, HC, T_ALL])
                        tt(mag[:, :, :], wide(al[:, :]), power, ALU.mult)
                        tt(turns[:, :, :], wide(t_hi), power, ALU.mult)
                        link(v.tensor_scalar(arg[:, :, :], turns[:, :, :], ROUND, ROUND, ALU.add, ALU.subtract))
                        tt(turns[:, :, :], turns[:, :, :], arg[:, :, :], ALU.subtract)
                        tt(arg[:, :, :], wide(sm(1)), power, ALU.mult)
                        tt(turns[:, :, :], turns[:, :, :], arg[:, :, :], ALU.add)
                        tt(turns[:, :, :], turns[:, :, :], off, ALU.add)
                        link(v.tensor_scalar(arg[:, :, :], turns[:, :, :], ROUND, ROUND, ALU.add, ALU.subtract))
                        v.tensor_tensor(arg[:, :, :], turns[:, :, :], arg[:, :, :], ALU.subtract).then_inc(args_ready, 1)
                        dve.wait_ge(sines_done, h + 1)
                        v.memset(stat[:, 0:1], 0.0).then_inc(mags_ready, 1)
                        dve.wait_ge(mags_done, h + 1)
                        tt(tab[:, hs, :], arg[:, :, 0:T_KEPT], mag[:, :, 0:T_KEPT], ALU.mult)
                        tt(vone[:, hs, :], arg[:, :, T_KEPT:], mag[:, :, T_KEPT:], ALU.mult)
                    o = T_ONE - T_KEPT
                    link(v.tensor_scalar(sm(3), vone[:, :, o], 1.0, None, ALU.subtract))
                    im = vone[:, :, o + 1]
                    tt(sm(4), al[:, :], al[:, :], ALU.mult)
                    tt(sm(5), sm(2), sm(2), ALU.mult)
                    tt(sm(4), sm(4), sm(5), ALU.add)
                    link(v.reciprocal(sm(4), sm(4)))
                    link(v.tensor_scalar(sm(4), sm(4), 2.0, None, ALU.mult))
                    tt(sm(5), sm(3), al[:, :], ALU.mult)
                    tt(sm(7), im, sm(2), ALU.mult)
                    tt(sm(5), sm(5), sm(7), ALU.add)
                    tt(sm(5), sm(5), sm(4), ALU.mult)
                    tt(sm(6), im, al[:, :], ALU.mult)
                    tt(sm(7), sm(3), sm(2), ALU.mult)
                    tt(sm(6), sm(6), sm(7), ALU.subtract)
                    tt(sm(6), sm(6), sm(4), ALU.mult)
                    f1, f2 = (sm(i).unsqueeze(2).to_broadcast([P, H, 8]) for i in (5, 6))
                    v1, v2 = vone[:, :, 0:8], vone[:, :, 8:16]
                    tmp = mag[:, :, :].rearrange("p a b -> p (a b)")[:, 0:8 * H].rearrange("p (a b) -> p a b", b=8)
                    tt(u1[:, :, :], f1, v1, ALU.mult)
                    tt(tmp, f2, v2, ALU.mult)
                    tt(u1[:, :, :], u1[:, :, :], tmp, ALU.add)
                    tt(u2[:, :, :], f1, v2, ALU.mult)
                    tt(tmp, f2, v1, ALU.mult)
                    tt(u2[:, :, :], u2[:, :, :], tmp, ALU.subtract)
                    link(v.tensor_reduce(qkv_bias[:, 0:G * D], bq_raw[:, :].rearrange("p (n j) -> p n j", j=J), AX_X, ALU.add))
                    for k in range(K):
                        dve.wait_ge(wq_in[k % 2], 16 * (k // 2 + 1))
                        v.tensor_reduce(wsum[:, k, 0:G * D], ring[:, k % 2, :].rearrange("p (n j) -> p n j", j=J),
                                        AX_X, ALU.add).then_inc(wq_summed, 1)
                        dve.wait_ge(wq_summed, k + 1)
                    dve.wait_ge(wkv_in, 16)
                    link(v.memset(stat[:, 0:1], 0.0))
                    v.memset(stat[:, 1:2], 0.0).then_inc(wsum_ready, 1)
                    dve.wait_ge(lora_in, 32)
                    tt(gate[:, 0:2], gate[:, 0:2], gate[:, 2:4], ALU.mult)
                    link(v.tensor_scalar(lora_a[:, 0, :], lora_a[:, 0, :], gate[:, 0:1], None, ALU.mult))
                    v.tensor_scalar(lora_a[:, 1, :], lora_a[:, 1, :], gate[:, 1:2], None, ALU.mult).then_inc(lora_scaled, 1)
                    dve.wait_ge(lora_scaled, 1)
                    dve.wait_ge(mean_done, 1)
                    mean = Q[:, :].rearrange("p (h n) -> p h n", h=2)[:, :, 0:384]
                    for k in range(K):
                        w = wsum[:, k, :].rearrange("p (h n) -> p h n", h=2)
                        v.tensor_tensor(w, w, mean, ALU.subtract).then_inc(centred, 1)
                        dve.wait_ge(centred, k + 1)
                    for k in range(K):
                        dve.wait_ge(w_hi_done, k + 1)
                        v.tensor_tensor(wl[:, k, :], wsum[:, k, :], wh[:, k, :].bitcast(F32), ALU.subtract).then_inc(w_split, 1)
                        dve.wait_ge(w_split, k + 1)
                    dve.wait_ge(wt_in, 16)
                    for k in range(K):
                        dve.wait_ge(lora_done, k + 1)
                        v.tensor_tensor(stage[:, k, :], stage[:, k, :], banks[k % 4][:, :], ALU.add).then_inc(merged, 1)
                        dve.wait_ge(merged, k + 1)
                    dve.wait_ge(fmean_done, 1)
                    for k in range(K):
                        v.tensor_tensor(stage[:, k, :], stage[:, k, :], T[:, :], ALU.subtract).then_inc(f_centred, 1)
                        dve.wait_ge(f_centred, k + 1)
                    for k in range(K):
                        dve.wait_ge(f_hi_done, k + 1)
                        link(v.tensor_tensor(fl[:, k, :], stage[:, k, :], fh[:, k, :].bitcast(F32), ALU.subtract))

        hh = [sb(f"hh{i}", [P, K, P], F32R) for i in range(2)]
        hl = [sb(f"hl{i}", [P, K, P], F32R) for i in range(2)]
        xr, xi = sb("xr", [P, R, C]), sb("xi", [P, R, C])
        pm, pt = sb("pm", [P, R, K, C]), sb("pt", [P, R, K, C])
        qm, qt = sb("qm", [P, R, 8, 16]), sb("qt", [P, R, 8, 16])
        htok = [sb(f"htok{i}", [P, K, P]) for i in range(2)]
        yo = sb("yo", [P, L])
        E = sb("E", [P, L])
        ET = sb("ET", [P, B * S, D])
        QA, KB = sb("QA", [P, B, R, D]), sb("KB", [P, B, S, D])
        kc = sb("kc", [P, B, D])
        qk, vs, vt = sb("qk", [P, QK]), sb("vs", [P, G * D]), sb("vt", [P, G, 32])
        VB = sb("VB", [P, B * S, R, GV])
        on, ot = sb("on", [P, G, 32]), sb("ot", [P, G * D])
        mx, rden = sb("mx", [P, B * S]), sb("rden", [P, B * R])
        bn = sb("bn", [P, 2, 12])
        var1, rs1, var2, rs2 = (stat[:, i + 4:i + 5] for i in range(4))
        mv1, mv2 = sb("mv1", [P, 2]), sb("mv2", [P, 2])

        names = """x_in powers_ready q_ready term_ready tok_done hi_done lo_done trans_done htok_ready
                 var1_ready rs1_ready  qk_done qk_evac v_done vt_ready vb_ready qk_written qa_in
                 k_in kb_ready s_done sub_done exp_done et_ready o_done ot_ready ott_done csum_done
                 c_ready hi2_done lo2_done var2_ready h2b_ready f0_done f1_done y0_done y_ready y_out
                 cls_out filled dve_passed sp_passed dve_chain act_chain pool_chain""".split()
        s = {n: sem(n) for n in names}
        LAST = GROUPS - 1

        def steps(eng, step, chain=None, per_pass=0):
            step(0, 0, False, True, True)
            step(1, 1, True, True, True)
            with eng.Fori(0, (LAST - 2) // 2) as i:
                if chain:
                    chain.enter(i, per_pass)
                for u in range(2):
                    step(2 * i + (2 + u), u, True, True, True)
            if chain:
                chain.leave((LAST - 2) // 2)
            step(LAST, LAST % 2, True, True, False)
            step(GROUPS, GROUPS % 2, True, False, False)

        xv = x.rearrange("(i n) m -> i n m", n=N)

        with nc.Block() as block:
            @block.sync
            def _(sp):
                def wait(name, count):
                    sp.wait_ge(s[name], count)
                    sp.sem_inc(s["sp_passed"])

                def step(j, u, back, front, ahead):
                    if ahead:
                        if back:
                            wait("powers_ready", j)
                            wait("term_ready", j)
                        for part, dst in enumerate((xr, xi)):
                            for half_ in range(2):
                                sp.dma_start(dst[N * half_:N * half_ + N, :, :].rearrange("p r c -> p (r c)"),
                                             xv[part, :, bass.ds(j * (R * C), R * C)]).then_inc(s["x_in"], 16)
                    if front:
                        wait("qk_evac", j + 1)
                        if not isinstance(j, int) or j >= 2:
                            wait("qa_in", 64 * (j - 1))
                            wait("k_in", 64 * (j - 1))
                        sp.dma_start(scratch[u].rearrange("i t n -> t i n"),
                                     qk[:, :].rearrange("p (i n) -> p i n", i=2)).then_inc(s["qk_written"], 16)
                        wait("qk_written", 16 * (j + 1))
                        sp.wait_ge(s["filled"], 1)
                        if back:
                            wait("s_done", j)
                            wait("kb_ready", j)
                        rows = lambda i, r: scratch[u][i, 32 * r:32 * r + 32, :].rearrange(
                            "(b s) (g d) -> (s g) b d", s=S, g=G)
                        for r in range(R):
                            sp.dma_start(kc[32 * r:32 * r + 32, :, :], rows(1, r)).then_inc(s["k_in"], 16)
                        for r in range(R):
                            sp.dma_start(QA[32 * r:32 * r + 32, :, r, :], rows(0, r)).then_inc(s["qa_in"], 16)
                    if back:
                        wait("y_ready", j)
                        if isinstance(j, int) and j == 1:
                            sp.dma_start(out[:, 0, :], yo[0:C, :]).then_inc(s["cls_out"], 16)
                        else:
                            for r in range(R):
                                sp.dma_start(out[:, bass.ds((j - 2) * R + (1 + r), 1), :].rearrange("c o n -> c (o n)"),
                                             yo[C * r:C * r + C, :]).then_inc(s["y_out"], 16)

                steps(sp, step)
                sp.wait_ge(s["cls_out"], 16)
                sp.wait_ge(s["y_out"], 64 * LAST)

            @block.gpsimd
            def _(pool):
                g = nc.gpsimd
                link = Chain(pool, s["pool_chain"])
                link(g.memset(QA[:, :, :, :].rearrange("p a b c -> p (a b c)"), 0.0))
                g.tensor_copy(VB[:, :, :, G], mask_r.unsqueeze(1).to_broadcast([P, B * S, R])).then_inc(s["filled"], 1)

                def step(j, u, back, front, ahead):
                    if back:
                        pool.wait_ge(s["lo_done"], j)
                        pool.wait_ge(s["hi_done"], j)
                        pool.wait_ge(s["et_ready"], j)
                        g.tensor_tensor(E[:, :], hh[1 - u][:, :, :].bitcast(F32).rearrange("p k n -> p (k n)"),
                                        hl[1 - u][:, :, :].bitcast(F32).rearrange("p k n -> p (k n)"), ALU.add).then_inc(s["csum_done"], 1)
                    if ahead:
                        if back:
                            pool.wait_ge(s["tok_done"], j)
                        p4 = bass.ds(j * R, R)
                        big = lambda at: tab[:, p4, at:at + 8].unsqueeze(3).to_broadcast([P, R, 8, 16])
                        low = lambda at: tab[:, p4, at:at + 16].unsqueeze(2).to_broadcast([P, R, 8, 16])
                        link(g.tensor_tensor(qm[:, :, :, :], big(T_AR), low(T_B1), ALU.mult))
                        link(g.tensor_tensor(qt[:, :, :, :], big(T_AI), low(T_B2), ALU.mult))
                        g.tensor_tensor(qm[:, :, :, :], qm[:, :, :, :], qt[:, :, :, :], ALU.add).then_inc(s["q_ready"], 1)
                        pool.wait_ge(s["q_ready"], j + 1)
                    if front:
                        pool.wait_ge(s["var1_ready"], j + 1)
                        g.tensor_tensor(rs1, var1, half[:, :], ALU.pow).then_inc(s["rs1_ready"], 1)
                    if ahead:
                        pool.wait_ge(s["x_in"], 64 * (j + 1))
                        if back:
                            pool.wait_ge(s["powers_ready"], j)
                        g.tensor_tensor(pt[:, :, :, :], xi[:, :, :].unsqueeze(2).to_broadcast([P, R, K, C]),
                                        u2[:, p4, :].unsqueeze(3).to_broadcast([P, R, K, C]), ALU.mult).then_inc(s["term_ready"], 1)
                    if back:
                        pool.wait_ge(s["var2_ready"], j)
                        link(g.tensor_tensor(rs2, var2, half[:, :], ALU.pow))
                        t = htok[1 - u][:, :, :].rearrange("p k a -> p (k a)")
                        g.tensor_tensor(t, t, ffn_bias[:, :], ALU.add).then_inc(s["h2b_ready"], 1)

                steps(pool, step, link, 2 * 3)

            @block.scalar
            def _(act):
                a_ = nc.scalar
                link = Chain(act, s["act_chain"])

                def step(j, u, back, front, ahead):
                    if front:
                        if back:
                            act.wait_ge(s["tok_done"], j)
                            if not isinstance(j, int) or j >= 2:
                                act.wait_ge(s["f1_done"], j - 1)
                            a_.activation(hh[u][:, :, :].rearrange("p k (r c) -> p r k c", r=R),
                                          T[:, :].rearrange("p (r k c) -> p r k c", r=R, k=K), ACT.Copy).then_inc(s["hi_done"], 1)
                        else:
                            a_.activation(hh[u][:, :, :], clst[:, :].unsqueeze(2).to_broadcast([P, K, P]), ACT.Copy).then_inc(s["hi_done"], 1)
                        act.wait_ge(s["trans_done"], j + 1)
                        if not isinstance(j, int) or j >= 2:
                            act.wait_ge(s["y_ready"], j - 1)
                        a_.activation(htok[u][:, :, :].rearrange("p k a -> p (k a)"), HT[:, :], ACT.Copy).then_inc(s["htok_ready"], 1)
                    if back:
                        act.wait_ge(s["c_ready"], j)
                        act.wait_ge(s["v_done"], j)
                        a_.activation(hh[1 - u][:, :, :].rearrange("p k n -> p (k n)"), E[:, :], ACT.Copy).then_inc(s["hi2_done"], 1)
                    if front:
                        act.wait_ge(s["vt_ready"], j + 1)
                        act.wait_ge(s["filled"], 1)
                        if back:
                            act.wait_ge(s["o_done"], j)
                        for r in range(R):
                            m = a_.activation(VB[:, :, r, 0:G], vt[:, :, :].rearrange("p g n -> p n g"), ACT.Copy, scale=mask_r[:, r:r + 1])
                            if r < R - 1:
                                link(m)
                        m.then_inc(s["vb_ready"], 1)
                        act.wait_ge(s["k_in"], 64 * (j + 1))
                        if back:
                            act.wait_ge(s["s_done"], j)
                        for q in range(S):
                            m = a_.activation(KB[:, :, q, :], kc[:, :, :], ACT.Copy, scale=mask_s[:, q:q + 1])
                            if q < S - 1:
                                link(m)
                        m.then_inc(s["kb_ready"], 1)
                        act.wait_ge(s["sub_done"], j + 1)
                        a_.activation(E[:, :], E[:, :], ACT.Exp, scale=float(D ** -0.5)).then_inc(s["exp_done"], 1)

                steps(act, step, link, 2 * 6)

            @block.tensor
            def _(pe):
                mm = nc.tensor.matmul

                def triple(dst, left, right, hi, lo, cols, stop_at=None):
                    for k in range(K):
                        for n, (a, w) in enumerate(((hi, left), (lo, left), (hi, right))):
                            m = mm(dst, a(k), w[:, k, cols], start=(k == 0 and n == 0), stop=(k == K - 1 and n == 2))
                    return m

                def step(j, u, back, front, ahead):
                    if front and back:
                        pe.wait_ge(s["powers_ready"], j)
                        pe.wait_ge(s["q_ready"], j)
                        pe.wait_ge(s["sub_done"], j)
                        for r in range(R):
                            m = mm(T[:, 256 * r:256 * r + 256], qm[:, r, :, :].rearrange("p a b -> p (a b)"),
                                   pm[:, r, :, :].rearrange("p k c -> p (k c)"), start=True, stop=True)
                        m.then_inc(s["tok_done"], 1)
                    if back:
                        pe.wait_ge(s["et_ready"], j)
                        pe.wait_ge(s["vb_ready"], j)
                        if not isinstance(j, int) or j >= 2:
                            pe.wait_ge(s["y0_done"], j - 1)
                        for n in range(B * S):
                            m = mm(O[32 * (n % S):32 * (n % S) + 32, n // S, :, :].rearrange("p r g -> p (r g)"),
                                   ET[:, n, :], VB[:, n, :, :].rearrange("p r g -> p (r g)"), start=True, stop=True)
                        m.then_inc(s["o_done"], 1)
                    if front:
                        pe.wait_ge(s["hi_done"], j + 1)
                        pe.wait_ge(s["lo_done"], j + 1)
                        if not isinstance(j, int) or j >= 2:
                            pe.wait_ge(s["var2_ready"], j - 1)
                            pe.wait_ge(s["c_ready"], j - 1)
                        for k in range(K):
                            for n, a in enumerate((hh[u], hl[u])):
                                m = mm(HT[:, P * k:P * k + P], a[:, k, :], identr[:, :], start=(n == 0), stop=(n == 1))
                        m.then_inc(s["trans_done"], 1)
                        plain = [lambda k, t=t: t[:, k, :] for t in (hh[u], hl[u])]
                        triple(Q[:, 0:QK], wh, wl, *plain, slice(0, QK)).then_inc(s["qk_done"], 1)
                    if back:
                        pe.wait_ge(s["ot_ready"], j)
                        if front:
                            pe.wait_ge(s["htok_ready"], j + 1)
                        mm(OTOK[:, :], perm, ot[:, :], start=True, stop=True)
                        for q in range(2):
                            m = mm(OT[:, q, :], ot[:, P * q:P * q + P], perm, start=True, stop=True)
                        m.then_inc(s["ott_done"], 1)
                    if front:
                        if back:
                            pe.wait_ge(s["vt_ready"], j)
                        triple(Q[:, QK:QKV], wh, wl, *plain, slice(QK, QKV)).then_inc(s["v_done"], 1)
                    if back:
                        pe.wait_ge(s["hi2_done"], j)
                        pe.wait_ge(s["lo2_done"], j)
                        turned = [lambda k, t=t: t[:, k, :] for t in (hh[1 - u], hl[1 - u])]
                        triple(F[:, 0:512], fh, fl, *turned, slice(0, 512)).then_inc(s["f0_done"], 1)
                    if front:
                        pe.wait_ge(s["qa_in"], 64 * (j + 1))
                        pe.wait_ge(s["kb_ready"], j + 1)
                        for b in range(B):
                            m = mm(T[:, P * b:P * b + P], QA[:, b, :, :].rearrange("p r d -> p (r d)"),
                                   KB[:, b, :, :].rearrange("p s e -> p (s e)"), start=True, stop=True)
                        m.then_inc(s["s_done"], 1)
                    if back:
                        if not isinstance(j, int) or j >= 2:
                            pe.wait_ge(s["y_ready"], j - 1)
                        triple(F[:, 512:1024], fh, fl, *turned, slice(512, 1024)).then_inc(s["f1_done"], 1)

                steps(pe, step)

            @block.vector
            def _(dve):
                v = nc.vector
                link = Chain(dve, s["dve_chain"])
                tt = lambda o, a, b, op: link(v.tensor_tensor(o, a, b, op))

                def signal(ins, name, count):
                    ins.then_inc(s[name], 1)
                    dve.wait_ge(s[name], count)

                def variance(t, stats, mv, var, name, count):
                    for n in range(2):
                        link(v.bn_stats(stats[:, 6 * n:6 * n + 6], t[:, 4 * n:4 * n + 4, :].rearrange("p k a -> p (k a)")))
                    dve.sem_inc(s["dve_passed"])
                    link(v.bn_aggr(mv[:, :], stats))
                    signal(v.tensor_scalar(var, mv[:, 1:2], EPS, None, ALU.add), name, count)

                def step(j, u, back, front, ahead):
                    if front:
                        dve.wait_ge(s["hi_done"], j + 1)
                        if back:
                            dve.wait_ge(s["tok_done"], j)
                            if not isinstance(j, int) or j >= 2:
                                dve.wait_ge(s["f1_done"], j - 1)
                            spread = lambda t: t[:, :, :].rearrange("p k (r c) -> p r k c", r=R)
                            signal(v.tensor_tensor(spread(hl[u]), T[:, :].rearrange("p (r k c) -> p r k c", r=R, k=K),
                                                   spread(hh[u]).bitcast(F32), ALU.subtract), "lo_done", j + 1)
                        else:
                            signal(v.tensor_tensor(hl[u][:, :, :], clst[:, :].unsqueeze(2).to_broadcast([P, K, P]),
                                                   hh[u][:, :, :].bitcast(F32), ALU.subtract), "lo_done", j + 1)
                    if back:
                        dve.wait_ge(s["o_done"], j)
                        link(v.reciprocal(rden[:, :].rearrange("p (b r) -> p b r", b=B), O[:, :, :, G]))
                        flat = F[:, 0:B * R * GV].rearrange("p (n g) -> p g n", g=GV)[:, 0:G, :]
                        tt(on[:, :, :], flat, rden[:, :].unsqueeze(1).to_broadcast([P, G, 32]), ALU.mult)
                        if not isinstance(j, int) or j >= 2:
                            dve.wait_ge(s["ott_done"], j - 1)
                        signal(v.transpose(ot[:, :].rearrange("p (q d gh) -> p gh q d", q=2, gh=4),
                                           on[:, :, :].rearrange("p (gh q) n -> p gh q n", q=2)), "ot_ready", j)
                    if front:
                        dve.wait_ge(s["htok_ready"], j + 1)
                        if back:
                            dve.wait_ge(s["rs1_ready"], j)
                        variance(htok[u], bn[:, 0, :], mv1, var1, "var1_ready", j + 1)
                    if back:
                        dve.wait_ge(s["ott_done"], j)
                        dve.wait_ge(s["csum_done"], j)
                        c = E[:, :].rearrange("p (q m n) -> p q m n", q=2, m=J)
                        signal(v.tensor_tensor(c, c, OT[:, :, :].unsqueeze(2).to_broadcast([P, 2, J, P]), ALU.add), "c_ready", j)
                        t = htok[1 - u]
                        c = t[:, :, :].rearrange("p (q m) a -> p q m a", q=2)
                        tt(c, c, OTOK.rearrange("p (q a) -> p q a", q=2).unsqueeze(2).to_broadcast([P, 2, J, P]), ALU.add)
                        if not isinstance(j, int) or j >= 2:
                            dve.wait_ge(s["h2b_ready"], j - 1)
                        variance(t, bn[:, 1, :], mv2, var2, "var2_ready", j)
                    if front:
                        dve.wait_ge(s["rs1_ready"], j + 1)
                        dve.wait_ge(s["qk_done"], j + 1)
                        if back:
                            dve.wait_ge(s["qk_written"], 16 * j)
                        signal(v.scalar_tensor_tensor(qk[:, :], Q[:, 0:QK], rs1, qkv_bias[:, 0:QK], ALU.mult, ALU.add), "qk_evac", j + 1)
                    if back:
                        dve.wait_ge(s["hi2_done"], j)
                        signal(v.tensor_tensor(hl[1 - u][:, :, :].rearrange("p k n -> p (k n)"), E[:, :],
                                               hh[1 - u][:, :, :].bitcast(F32).rearrange("p k n -> p (k n)"), ALU.subtract), "lo2_done", j)
                    if front:
                        dve.wait_ge(s["v_done"], j + 1)
                        link(v.scalar_tensor_tensor(vs[:, :], Q[:, QK:QKV], rs1, qkv_bias[:, QK:QKV], ALU.mult, ALU.add))
                        if back:
                            dve.wait_ge(s["vb_ready"], j)
                        signal(v.transpose(vt[:, :, :].rearrange("p g n -> p (g n)"), vs[:, :]), "vt_ready", j + 1)
                    if ahead:
                        dve.wait_ge(s["x_in"], 64 * (j + 1))
                        if back:
                            dve.wait_ge(s["tok_done"], j)
                        tt(pm[:, :, :, :], xr[:, :, :].unsqueeze(2).to_broadcast([P, R, K, C]),
                           u1[:, bass.ds(j * R, R), :].unsqueeze(3).to_broadcast([P, R, K, C]), ALU.mult)
                        dve.wait_ge(s["term_ready"], j + 1)
                        signal(v.tensor_tensor(pm[:, :, :, :], pm[:, :, :, :], pt[:, :, :, :], ALU.add), "powers_ready", j + 1)

                    def rows(n):
                        at = slice(512 * n, 512 * n + 512)
                        return v.scalar_tensor_tensor(
                            yo[:, at].rearrange("p (a k) -> p a k", k=K), F[:, at].rearrange("p (a k) -> p a k", k=K), rs2,
                            htok[1 - u][:, :, 64 * n:64 * n + 64].rearrange("p k a -> p a k"), ALU.mult, ALU.add)

                    if back:
                        dve.wait_ge(s["f0_done"], j)
                        dve.wait_ge(s["h2b_ready"], j)
                        if not isinstance(j, int) or j >= 2:
                            dve.wait_ge(s["cls_out"], 16)
                        if not isinstance(j, int) or j >= 3:
                            dve.wait_ge(s["y_out"], 64 * (j - 2))
                        signal(rows(0), "y0_done", j)
                    if front:
                        dve.wait_ge(s["s_done"], j + 1)
                        sc = T[:, :].rearrange("p (n e) -> p n e", e=D)
                        link(v.tensor_reduce(mx[:, :], sc, AX_X, ALU.max))
                        if back:
                            dve.wait_ge(s["lo2_done"], j)
                        signal(v.tensor_tensor(E[:, :].rearrange("p (n e) -> p n e", e=D), sc,
                                               mx[:, :].unsqueeze(2).to_broadcast([P, B * S, D]), ALU.subtract), "sub_done", j + 1)
                        dve.wait_ge(s["exp_done"], j + 1)
                        signal(v.transpose(ET[:, :, :].rearrange("p n d -> p (n d)"), E[:, :]), "et_ready", j + 1)
                    if back:
                        dve.wait_ge(s["f1_done"], j)
                        signal(rows(1), "y_ready", j)

                steps(dve, step, link, 2 * (2 + 3 + 1 + 3 + 1 + 1 + 1))


def _flat(a):
    return np.ascontiguousarray(a)


def kernel(x, cls_tok, L0_tok_A_abslog, L0_tok_A_phase, L0_attn_Wq, L0_attn_bq, L0_attn_Wk, L0_attn_bk,
           L0_attn_Wv, L0_attn_bv, L0_ffn_W, L0_ffn_bias, L0_ffn_A, L0_ffn_Bf, L0_ffn_coeffs, L0_ffn_scales):
    import concourse.bacc as bacc
    from concourse.bass_utils import run_bass_kernel_spmd

    def by_group(w):
        w = np.asarray(w)
        w = w.reshape(*w.shape[:-1], G, w.shape[-1] // G)
        w = np.moveaxis(w, -2, -3)
        return w.reshape(*w.shape[:-3], -1)

    chunked = lambda w: np.moveaxis(w.reshape(*w.shape[:-1], P, K), -1, -2).reshape(*w.shape[:-1], L)
    arrays = {
        "x": _flat(np.transpose(np.asarray(x), (3, 2, 1, 0)).reshape(2 * N, H * C)),
        "alog": _flat(np.asarray(L0_tok_A_abslog).T),
        "phase": _flat(np.asarray(L0_tok_A_phase).T),
        "cls": _flat(np.asarray(cls_tok).reshape(L)),
        "wq": _flat(by_group(L0_attn_Wq)),
        "wkv": _flat(np.concatenate([by_group(L0_attn_Wk), by_group(L0_attn_Wv)], -1)),
        "bq": _flat(by_group(L0_attn_bq)),
        "bkv": _flat(np.concatenate([by_group(L0_attn_bk), by_group(L0_attn_bv)], -1)),
        "wt": _flat(np.asarray(L0_ffn_W).T),
        "fbias": _flat(chunked(np.asarray(L0_ffn_bias))),
        "fa": _flat(chunked(np.asarray(L0_ffn_A).reshape(ER, L))),
        "fb": _flat(np.transpose(np.asarray(L0_ffn_Bf), (0, 2, 1)).reshape(ER, L)),
        "gates": _flat(np.concatenate([np.repeat(np.asarray(a), 16).reshape(2, P)
                                       for a in (L0_ffn_coeffs, L0_ffn_scales)]).T),
        "const": constants(),
    }
    nc = bacc.Bacc("TRN2", target_bir_lowering=False, num_devices=1)
    ins = [nc.dram_tensor(f"in_{n}", a.shape, mybir.dt.from_np(a.dtype), kind="ExternalInput").ap()
           for n, a in arrays.items()]
    y = nc.dram_tensor("out_rows", (C, H + 1, L), F32, kind="ExternalOutput").ap()
    tower(nc, *ins, y)
    r = run_bass_kernel_spmd(nc, [{f"in_{n}": a for n, a in arrays.items()}], core_ids=[0])
    return r.results[0]["out_rows"]
```

```python
from contextlib import ExitStack

import concourse.bass as bass
import numpy as np
from concourse import mybir

ALU = mybir.AluOpType
ACT = mybir.ActivationFunctionType
AX_X = mybir.AxisListType.X
F32 = mybir.dt.float32
F32R = mybir.dt.float32r

P = 128
C, H, N, L = 32, 64, 64, 1024
K = L // P
R, S, B = 4, 4, 8
D, G, J = 32, 8, 4
QK = 2 * G * D
QKV = 3 * G * D
ER = 256
GROUPS = 1 + H // R
GV = G + 1
EPS = 1e-5

T_B1, T_B2, T_AR, T_AI, T_ALL = 0, 16, 32, 40, 48
Z_B, Z_A, Z_V, Z_ALL = 0, 16, 24, 32
HALVES = 2
RING = 4
RING = 4
LORA_BANKS = 3
W_PARTS = ["keys and values, 0", "keys and values, 1", "queries"]
WEIGHT_ORDER = [0, 1, 2, *W_PARTS[:2], 3, W_PARTS[2], 4, 5, 6, 7]

C_ID, C_PERM, C_MV, C_MQ, C_MK, C_POW = 0, 128, 256, 260, 264, 268
C_OFF = C_POW + Z_ALL
C_ALL = C_OFF + 1
ROUND = 1.5 * 2.0 ** 23
INV_HI = float(np.floor(2.0 ** 14 / (2 * np.pi)) / 2.0 ** 14)
INV_LO = float(1 / (2 * np.pi) - INV_HI)
TWO_PI = 6.283185


def constants():
    c = np.zeros((P, C_ALL), np.float32)
    p = np.arange(P)
    c[p, C_ID + p] = 1
    r, s, b = p // 32, p % 32 // 8, p % 8
    c[32 * s + 4 * b + r, C_PERM + p] = 1
    c[p, C_MV + p // 32] = 1
    c[p, C_MQ + p % 16 // 4] = 1
    c[p, C_MK + p % 4] = 1
    c[:, C_POW + Z_B:C_POW + Z_A] = 8 * np.arange(16)
    c[:, C_POW + Z_A:C_POW + Z_V] = 128 * np.arange(8)
    c[:, C_POW + Z_V:C_POW + Z_ALL] = np.arange(8)
    c[:N, C_OFF] = 0.25
    return c


def part_maps():
    m = np.zeros((P, 5, P), np.float32)
    n = np.arange(N)
    for i, ((top, top_sign), (low, low_sign)) in enumerate([
            ((1, -1), (0, 1)), ((0, 1), (0, 1)), ((1, 1), (1, 1)), ((0, 1), (1, -1)), ((1, -1), (0, -1))]):
        m[N * top + n, i, n] = top_sign
        m[N * low + n, i, N + n] = low_sign
    return m


class Chain:

    def __init__(self, eng, sem):
        self.eng, self.sem, self.n, self.past = eng, sem, 0, 0

    def __call__(self, ins):
        self.n += 1
        ins.then_inc(self.sem, 1)
        self.eng.wait_ge(self.sem, self.past + self.n)

    def enter(self, i, per_pass):
        self.past, self.at, self.per_pass = i * per_pass, self.n, per_pass

    def leave(self, passes):
        assert self.n - self.at == self.per_pass, (self.n - self.at, self.per_pass)
        self.n, self.past = self.at + passes * self.per_pass, 0


def tower(nc, x, modes, cls, wq, wkv, bq, bkv, wt, fbias, fa, fb, gates, const, maps, out):
    ctx = ExitStack()
    with ctx:
        sem = lambda name: ctx.enter_context(nc.semaphore(name))

        def sb(name, shape, dt=F32, into=ctx):
            return into.enter_context(nc.sbuf_tensor(name, shape, dt))

        with ExitStack() as under_wh:
            ring = sb("ring", [P, RING, L], F32, under_wh)
            part = sb("part", [P, 5, P], F32, under_wh)
            bq_raw = sb("bq_raw", [P, L], F32, under_wh)
        wh = sb("wh", [P, K, QKV], F32R)
        with ExitStack() as under_wl:
            wsum = sb("wsum", [P, K, QKV], F32, under_wl)
        wl = sb("wl", [P, K, QKV], F32R)
        fh = sb("fh", [P, K, L], F32R)
        with ExitStack() as under_fl:
            stage = sb("stage", [P, K, L], F32, under_fl)
        fl = sb("fl", [P, K, L], F32R)
        tab = sb("tab", [P, H, T_ALL])
        u1, u2 = sb("u1", [P, H, 8]), sb("u2", [P, H, 8])
        cst = sb("cst", [P, C_ALL])
        identr = sb("identr", [P, P], F32R)
        qkv_bias, ffn_bias = sb("qkv_bias", [P, QKV]), sb("ffn_bias", [P, L])
        clst = sb("clst", [P, K])
        stat = sb("stat", [P, 16])
        half = sb("half", [P, 1])
        perm = cst[:, C_PERM:C_PERM + P]
        mask_v = cst[:, C_MV:C_MV + R]
        mask_q = cst[:, C_MQ:C_MQ + R]
        mask_k = cst[:, C_MK:C_MK + S]

        T = ctx.enter_context(nc.psum_tensor("T", [P, L], F32))
        Q = ctx.enter_context(nc.psum_tensor("Q", [P, L], F32))
        HT = ctx.enter_context(nc.psum_tensor("HT", [P, L], F32))
        F = ctx.enter_context(nc.psum_tensor("F", [P, L], F32))
        O = F[:, 0:B * R * GV].rearrange("p (b r g) -> p b r g", b=B, r=R)
        OTOK = F[:, 512:768]
        OT = F[:, 768:1024].rearrange("p (q n) -> p q n", q=2)

        scratch = [nc.dram_tensor(f"qk_scratch{i}", (2, G, P, D), F32, kind="Internal").ap()
                   for i in range(2)]

        with ExitStack() as early:
            lora_a, lora_b = sb("lora_a", [P, 2, L], F32, early), sb("lora_b", [P, 2, L], F32, early)
            arg, turns, mag, rest = (sb(n, [P, H, Z_ALL], F32, early) for n in ("arg", "turns", "mag", "rest"))
            mode, small = sb("mode", [P, 2, H], F32, early), sb("small", [P, 8, H], F32, early)
            phr = sb("phr", [P, 2, H], F32R, early)
            ksum = sb("ksum", [P, 2, L], F32, early)
            ksum_hi, ksum_lo = sb("ksum_hi", [P, L], F32R, early), sb("ksum_lo", [P, L], F32R, early)
            ones, minus = sb("ones", [P, P], F32, early), sb("minus", [P, P], F32R, early)
            gate = sb("gate", [P, 8], F32, early)
            ph, al = mode[:, 0, :], mode[:, 1, :]
            vv = mag[:, :, :].rearrange("p h n -> p (h n)")[:, 0:2 * 8 * H].rearrange("p (i h b) -> p i h b", i=2, h=H)

            modes_in, a_in, b_in, small_in = sem("modes_in"), sem("a_in"), sem("b_in"), sem("small_in")
            wt_in = [sem(f"wt_in{i}") for i in range(2)]
            wkv_in = sem("wkv_in")
            wq_in = [sem(f"wq_in{i}") for i in range(RING)]
            dve0, pool0 = sem("dve_setup"), sem("pool_setup")
            phases_ready, rest_ready, args_ready, mags_ready = (
                sem(n) for n in ("phases_ready", "rest_ready", "args_ready", "mags_ready"))
            sines_done, mags_done, base_ready = sem("sines_done"), sem("mags_done"), sem("base_ready")
            mapped, swapped_copied, parts_copied, v_copied, z_mapped, z_read = (
                sem(n) for n in ("mapped", "swapped_copied", "parts_copied", "v_copied", "z_mapped", "z_read"))
            lora_scaled, ones_ready, half_sum, ksum_ready, ksum_hi_ready, ksum_split = (
                sem(n) for n in ("lora_scaled", "ones_ready", "half_sum", "ksum_ready", "ksum_hi_ready", "ksum_split"))
            lora_done, merged, f_hi_done, f_lo_done = (sem(n) for n in ("lora_done", "merged", "f_hi_done", "f_lo_done"))
            wq_summed, kv_mean, q_mean, centred, w_hi_done = (
                sem(n) for n in ("wq_summed", "kv_mean", "q_mean", "centred", "w_hi_done"))
            banks = [T, Q, HT]
            GD = G * D
            halves = [slice(H // HALVES * i, H // HALVES * (i + 1)) for i in range(HALVES)]
            w_parts = [(slice(0, K // 2), slice(GD, QKV)), (slice(K // 2, K), slice(GD, QKV)), (slice(0, K), slice(0, GD))]

            with nc.Block() as block:
                @block.sync
                def _(sp):
                    for i in range(2):
                        sp.dma_start(mode[N * i:N * i + N, :, :], modes).then_inc(modes_in, 16)
                    sp.dma_start(cst[:, :], const).then_inc(modes_in, 16)
                    sp.dma_start(gate[:, 0:4], gates).then_inc(a_in, 16)
                    sp.dma_start(lora_a[:, :, :], fa.rearrange("(q p) n -> p q n", p=P)).then_inc(a_in, 16)
                    sp.dma_start(lora_b[:, :, :], fb.rearrange("(q p) n -> p q n", p=P)).then_inc(b_in, 16)
                    for i in range(2):
                        ks = slice(K // 2 * i, K // 2 * (i + 1))
                        sp.dma_start(stage[:, ks, :], wt.rearrange("(a k) n -> a k n", k=K)[:, ks, :]).then_inc(wt_in[i], 16)
                    sp.dma_start(part[:, :, :], maps).then_inc(small_in, 16)
                    sp.dma_start(wsum[:, :, GD:], wkv.rearrange("(a k) n -> a k n", k=K)).then_inc(wkv_in, 16)
                    for k in range(K):
                        if k >= RING:
                            sp.wait_ge(wq_summed, k - RING + 1)
                        sp.dma_start(ring[:, k % RING, :], wq.rearrange("(a k) n -> a k n", k=K)[:, k, :]).then_inc(wq_in[k % RING], 16)
                    sp.dma_start(clst[:, :], cls.rearrange("(a k) -> a k", k=K)).then_inc(small_in, 16)
                    sp.dma_start(bq_raw[:, :], bq.partition_broadcast(P)).then_inc(small_in, 16)
                    sp.dma_start(qkv_bias[:, GD:], bkv.partition_broadcast(P)).then_inc(small_in, 16)
                    sp.dma_start(ffn_bias[:, :], fbias.partition_broadcast(P)).then_inc(small_in, 16)

                @block.gpsimd
                def _(pool):
                    g = nc.gpsimd
                    link = Chain(pool, pool0)
                    pool.wait_ge(modes_in, 3 * 16)
                    power = cst[:, C_POW:C_POW + Z_ALL].unsqueeze(1).to_broadcast([P, H // HALVES, Z_ALL])
                    wide = lambda a, hs: a[:, hs].unsqueeze(2).to_broadcast([P, H // HALVES, Z_ALL])
                    pool.wait_ge(phases_ready, 1)
                    for hs in halves:
                        g.tensor_tensor(rest[:, hs, :], wide(small[:, 1, :], hs), power, ALU.mult).then_inc(rest_ready, 1)
                    for hs in halves:
                        g.tensor_tensor(mag[:, hs, :], wide(al, hs), power, ALU.mult).then_inc(mags_ready, 1)
                    pool.wait_ge(wt_in[0], 16)
                    link(g.tensor_tensor(ksum[:, 0, :], stage[:, 0, :], stage[:, 1, :], ALU.add))
                    for k in range(2, K // 2):
                        link(g.tensor_tensor(ksum[:, 0, :], ksum[:, 0, :], stage[:, k, :], ALU.add))
                    pool.wait_ge(half_sum, 1)
                    g.tensor_tensor(ksum[:, 0, :], ksum[:, 0, :], ksum[:, 1, :], ALU.add).then_inc(ksum_ready, 1)
                    pool.wait_ge(ksum_hi_ready, 1)
                    g.tensor_tensor(ksum_lo[:, :], ksum[:, 0, :], ksum_hi[:, :].bitcast(F32), ALU.subtract).then_inc(ksum_split, 1)
                    for k in range(0, K, 2):
                        if k == 4:
                            for i in range(2):
                                ks, at = w_parts[i]
                                pool.wait_ge(w_hi_done, i + 1)
                                link(g.tensor_tensor(wl[:, ks, at], wsum[:, ks, at], wh[:, ks, at].bitcast(F32), ALU.subtract))
                        pool.wait_ge(f_hi_done, k + 1)
                        link(g.tensor_tensor(fl[:, k, :], stage[:, k, :], fh[:, k, :].bitcast(F32), ALU.subtract))

                @block.scalar
                def _(act):
                    for i, hs in enumerate(halves):
                        act.wait_ge(args_ready, i + 1)
                        nc.scalar.activation(arg[:, hs, :], arg[:, hs, :], ACT.Sin, scale=TWO_PI).then_inc(sines_done, 1)
                    for i, hs in enumerate(halves):
                        act.wait_ge(mags_ready, i + 1)
                        nc.scalar.activation(mag[:, hs, :], mag[:, hs, :], ACT.Exp).then_inc(mags_done, 1)
                    act.wait_ge(ksum_ready, 1)
                    nc.scalar.activation(ksum_hi[:, :], ksum[:, 0, :], ACT.Copy).then_inc(ksum_hi_ready, 1)
                    act.wait_ge(mapped, 1)
                    nc.scalar.activation(tab[:, :, T_B2:T_AR], HT[:, :].rearrange("p (h b) -> p h b", h=H), ACT.Copy).then_inc(swapped_copied, 1)
                    act.wait_ge(mapped, 2)
                    act.wait_ge(mags_done, HALVES)
                    act.wait_ge(base_ready, 1)
                    nc.scalar.activation(vv, F[:, :].rearrange("p (i h b) -> p i h b", i=2, h=H), ACT.Copy).then_inc(v_copied, 1)
                    act.wait_ge(mapped, 3)
                    nc.scalar.activation(tab[:, :, T_AR:].rearrange("p h (i a) -> p i h a", i=2),
                                         HT[:, :].rearrange("p (i h a) -> p i h a", i=2, h=H), ACT.Copy).then_inc(parts_copied, 1)
                    for n in WEIGHT_ORDER:
                        if isinstance(n, str):
                            i = W_PARTS.index(n)
                            ks, at = w_parts[i]
                            act.wait_ge(centred, i + 1)
                            act.wait_ge(wq_summed, K + 1)
                            act.wait_ge(mapped, 3)
                            nc.scalar.activation(wh[:, ks, at], wsum[:, ks, at], ACT.Copy).then_inc(w_hi_done, 1)
                        else:
                            act.wait_ge(merged, n + 1)
                            nc.scalar.activation(fh[:, n, :], stage[:, n, :], ACT.Copy).then_inc(f_hi_done, 1)

                @block.tensor
                def _(pe):
                    mm = nc.tensor.matmul

                    def experts(k):
                        for o in range(2):
                            for q in range(2):
                                m = mm(banks[k % LORA_BANKS][:, 512 * o:512 * o + 512], lora_a[:, q, P * k:P * k + P],
                                       lora_b[:, q, 512 * o:512 * o + 512], start=(q == 0), stop=False)

                    def less_mean(k):
                        for o in range(2):
                            for n, t in enumerate((ksum_hi, ksum_lo)):
                                m = mm(banks[k % LORA_BANKS][:, 512 * o:512 * o + 512], minus[:, :], t[:, 512 * o:512 * o + 512],
                                       start=False, stop=(n == 1))
                        m.then_inc(lora_done, 1)

                    pe.wait_ge(ones_ready, 2)
                    pe.wait_ge(lora_scaled, 2)
                    pe.wait_ge(b_in, 16)
                    experts(0)
                    experts(1)
                    pe.wait_ge(small_in, 16)
                    pe.wait_ge(base_ready, 1)
                    for o in range(2):
                        m = mm(HT[:, 512 * o:512 * o + 512], part[:, 0, :], tab[:, 32 * o:32 * o + 32, T_B1:T_B2], start=True, stop=True)
                    m.then_inc(mapped, 1)
                    for o in range(2):
                        m = mm(F[:, 512 * o:512 * o + 512], part[:, 3 + o, :], arg[:, :, Z_V:], start=True, stop=True)
                    m.then_inc(mapped, 1)
                    pe.wait_ge(swapped_copied, 1)
                    for o in range(2):
                        m = mm(HT[:, 512 * o:512 * o + 512], part[:, 1 + o, :], arg[:, :, Z_A:Z_V], start=True, stop=True)
                    m.then_inc(mapped, 1)
                    pe.wait_ge(v_copied, 1)
                    for o in range(2):
                        m = mm(F[:, 512 * o:512 * o + H], part[:, 1 + o, :], arg[:, :, Z_V + 1], start=True, stop=True)
                    m.then_inc(z_mapped, 1)
                    pe.wait_ge(ksum_hi_ready, 1)
                    pe.wait_ge(ksum_split, 1)
                    less_mean(0)
                    less_mean(1)
                    pe.wait_ge(parts_copied, 1)
                    experts(2)
                    less_mean(2)
                    pe.wait_ge(z_read, 1)
                    pe.wait_ge(wkv_in, 16)
                    for k in range(K):
                        m = mm(F[:, 0:2 * GD], ones[:, :], wsum[:, k, GD:], start=(k == 0), stop=(k == K - 1))
                    m.then_inc(kv_mean, 1)
                    for k in range(LORA_BANKS, K):
                        pe.wait_ge(merged, k - LORA_BANKS + 1)
                        experts(k)
                        less_mean(k)
                        if k == LORA_BANKS:
                            pe.wait_ge(wq_summed, K)
                            for q in range(K):
                                m = mm(F[:, 2 * GD:3 * GD], ones[:, :], wsum[:, q, 0:GD], start=(q == 0), stop=(q == K - 1))
                            m.then_inc(q_mean, 1)

                @block.vector
                def _(dve):
                    v = nc.vector
                    link = Chain(dve, dve0)
                    tt = lambda o, a, b, op: link(v.tensor_tensor(o, a, b, op))
                    sm = lambda i: small[:, i, :]
                    link(v.memset(half[:, :], -0.5))
                    link(v.memset(ones[:, :], -1.0 / L))
                    v.tensor_copy(minus[:, :], ones[:, :]).then_inc(ones_ready, 1)
                    dve.wait_ge(ones_ready, 1)
                    v.memset(ones[:, :], 1.0 / L).then_inc(ones_ready, 1)
                    dve.wait_ge(modes_in, 3 * 16)
                    link(v.tensor_copy(phr[:, 0, :], ph))
                    p_hi = phr[:, 0, :].bitcast(F32)
                    t_hi = phr[:, 1, :].bitcast(F32)
                    tt(sm(0), ph, p_hi, ALU.subtract)
                    link(v.tensor_scalar(sm(1), p_hi, INV_HI, None, ALU.mult))
                    link(v.tensor_copy(phr[:, 1, :], sm(1)))
                    tt(sm(1), sm(1), t_hi, ALU.subtract)
                    link(v.scalar_tensor_tensor(sm(1), p_hi, INV_LO, sm(1), ALU.mult, ALU.add))
                    v.scalar_tensor_tensor(sm(1), sm(0), INV_HI + INV_LO, sm(1), ALU.mult, ALU.add).then_inc(phases_ready, 1)
                    dve.wait_ge(phases_ready, 1)
                    dve.wait_ge(a_in, 2 * 16)
                    tt(gate[:, 0:2], gate[:, 0:2], gate[:, 2:4], ALU.mult)
                    link(v.tensor_reduce(gate[:, 4:6], lora_a[:, :, :], AX_X, ALU.add))
                    link(v.tensor_scalar(gate[:, 4:6], gate[:, 4:6], 1.0 / L, None, ALU.mult))
                    for q in range(2):
                        v.tensor_scalar(lora_a[:, q, :], lora_a[:, q, :], gate[:, 4 + q:5 + q], gate[:, q:q + 1],
                                        ALU.subtract, ALU.mult).then_inc(lora_scaled, 1)
                    off = cst[:, C_OFF:C_OFF + 1]
                    power = cst[:, C_POW:C_POW + Z_ALL].unsqueeze(1).to_broadcast([P, H // HALVES, Z_ALL])
                    for i, hs in enumerate(halves):
                        t, a = turns[:, hs, :], arg[:, hs, :]
                        tt(t, t_hi[:, hs].unsqueeze(2).to_broadcast([P, H // HALVES, Z_ALL]), power, ALU.mult)
                        link(v.tensor_scalar(a, t, ROUND, ROUND, ALU.add, ALU.subtract))
                        tt(t, t, a, ALU.subtract)
                        dve.wait_ge(rest_ready, i + 1)
                        link(v.scalar_tensor_tensor(t, t, off, rest[:, hs, :], ALU.add, ALU.add))
                        link(v.tensor_scalar(a, t, ROUND, ROUND, ALU.add, ALU.subtract))
                        v.tensor_tensor(a, t, a, ALU.subtract).then_inc(args_ready, 1)
                    dve.wait_ge(wt_in[1], 16)
                    tt(ksum[:, 1, :], stage[:, K // 2, :], stage[:, K // 2 + 1, :], ALU.add)
                    tt(ksum[:, 1, :], ksum[:, 1, :], stage[:, K // 2 + 2, :], ALU.add)
                    v.tensor_tensor(ksum[:, 1, :], ksum[:, 1, :], stage[:, K - 1, :], ALU.add).then_inc(half_sum, 1)
                    for i, hs in enumerate(halves):
                        dve.wait_ge(sines_done, i + 1)
                        dve.wait_ge(mags_done, i + 1)
                        link(v.tensor_tensor(tab[:, hs, T_B1:T_B2], arg[:, hs, Z_B:Z_A], mag[:, hs, Z_B:Z_A], ALU.mult))
                        m = v.tensor_tensor(arg[:, hs, Z_A:], arg[:, hs, Z_A:], mag[:, hs, Z_A:], ALU.mult)
                        if i < HALVES - 1:
                            link(m)
                    m.then_inc(base_ready, 1)

                    def sum_wq(k):
                        dve.wait_ge(wq_in[k % RING], 16 * (k // RING + 1))
                        v.tensor_reduce(wsum[:, k, 0:GD], ring[:, k % RING, :].rearrange("p (n j) -> p n j", j=J),
                                        AX_X, ALU.add).then_inc(wq_summed, 1)

                    for k in range(4):
                        sum_wq(k)
                    link(v.tensor_scalar(sm(2), t_hi, ROUND, ROUND, ALU.add, ALU.subtract))
                    tt(sm(2), t_hi, sm(2), ALU.subtract)
                    tt(sm(2), sm(2), sm(1), ALU.add)
                    link(v.tensor_scalar(sm(3), sm(2), ROUND, ROUND, ALU.add, ALU.subtract))
                    tt(sm(2), sm(2), sm(3), ALU.subtract)
                    link(v.tensor_scalar(sm(2), sm(2), float(2 * np.pi), None, ALU.mult))
                    tt(sm(4), al, al, ALU.mult)
                    tt(sm(5), sm(2), sm(2), ALU.mult)
                    tt(sm(4), sm(4), sm(5), ALU.add)
                    link(v.reciprocal(sm(4), sm(4)))
                    link(v.tensor_scalar(sm(4), sm(4), 2.0, None, ALU.mult))
                    dve.wait_ge(z_mapped, 1)
                    link(v.tensor_scalar(sm(3), F[:, 0:H], 1.0, None, ALU.subtract))
                    im = sm(0)
                    v.tensor_copy(im, F[:, 512:512 + H]).then_inc(z_read, 1)
                    dve.wait_ge(z_read, 1)
                    tt(sm(5), sm(3), al, ALU.mult)
                    tt(sm(7), im, sm(2), ALU.mult)
                    tt(sm(5), sm(5), sm(7), ALU.add)
                    tt(sm(5), sm(5), sm(4), ALU.mult)
                    tt(sm(6), im, al, ALU.mult)
                    tt(sm(7), sm(3), sm(2), ALU.mult)
                    tt(sm(6), sm(6), sm(7), ALU.subtract)
                    tt(sm(6), sm(6), sm(4), ALU.mult)
                    for k in range(4, K):
                        sum_wq(k)
                    dve.wait_ge(small_in, 5 * 16)
                    v.tensor_reduce(qkv_bias[:, 0:GD], bq_raw[:, :].rearrange("p (n j) -> p n j", j=J), AX_X, ALU.add).then_inc(wq_summed, 1)

                    def f_lo(k):
                        dve.wait_ge(f_hi_done, k + 1)
                        link(v.tensor_tensor(fl[:, k, :], stage[:, k, :], fh[:, k, :].bitcast(F32), ALU.subtract))

                    for n in WEIGHT_ORDER:
                        if isinstance(n, str):
                            i = W_PARTS.index(n)
                            ks, at = w_parts[i]
                            dve.wait_ge(kv_mean if i < 2 else q_mean, 1)
                            mean = F[:, at.start - GD:at.stop - GD] if i < 2 else F[:, 2 * GD:3 * GD]
                            w = wsum[:, ks, at]
                            v.tensor_tensor(w, w, mean.unsqueeze(1).to_broadcast(list(w.shape)), ALU.subtract).then_inc(centred, 1)
                        else:
                            dve.wait_ge(lora_done, n + 1)
                            v.tensor_tensor(stage[:, n, :], stage[:, n, :], banks[n % LORA_BANKS][:, :], ALU.add).then_inc(merged, 1)
                        if isinstance(n, int) and n >= 2 and n % 2 == 0:
                            f_lo(n - 1)
                    f_lo(K - 1)
                    ks, at = w_parts[2]
                    dve.wait_ge(w_hi_done, 3)
                    link(v.tensor_tensor(wl[:, ks, at], wsum[:, ks, at], wh[:, ks, at].bitcast(F32), ALU.subtract))
                    link(v.tensor_copy(identr[:, :], cst[:, C_ID:C_ID + P]))
                    dve.wait_ge(v_copied, 1)
                    f1, f2 = (sm(i).unsqueeze(2).to_broadcast([P, H, 8]) for i in (5, 6))
                    v1, v2 = vv[:, 0, :, :], vv[:, 1, :, :]
                    tmp = rest[:, :, 0:8]
                    tt(u1[:, :, :], f1, v1, ALU.mult)
                    tt(tmp, f2, v2, ALU.mult)
                    tt(u1[:, :, :], u1[:, :, :], tmp, ALU.add)
                    tt(u2[:, :, :], f1, v2, ALU.mult)
                    tt(tmp, f2, v1, ALU.mult)
                    tt(u2[:, :, :], u2[:, :, :], tmp, ALU.subtract)

        hh = [sb(f"hh{i}", [P, K, P], F32R) for i in range(2)]
        hl = [sb(f"hl{i}", [P, K, P], F32R) for i in range(2)]
        xc = sb("xc", [P, 2, R * C])
        xr, xi = (xc[:, i, :].rearrange("p (r c) -> p r c", r=R) for i in range(2))
        pm, pt = sb("pm", [P, R, K, C]), sb("pt", [P, R, K, C])
        qm, qt = sb("qm", [P, R, 8, 16]), sb("qt", [P, R, 8, 16])
        htok = [sb(f"htok{i}", [P, K, P]) for i in range(2)]
        yo = sb("yo", [P, L])
        E = sb("E", [P, L])
        ET = sb("ET", [P, B * S, D])
        QA, KB = sb("QA", [P, B, R, D]), sb("KB", [P, B, S, D])
        qkc = sb("qkc", [P, 2, B, D])
        qk, vs, vt = sb("qk", [P, QK]), sb("vs", [P, G * D]), sb("vt", [P, G, 32])
        VB = sb("VB", [P, B * S, R, GV])
        on, ot = sb("on", [P, G, 32]), sb("ot", [P, G * D])
        mx, rden = sb("mx", [P, B * S]), sb("rden", [P, B * R])
        bn = sb("bn", [P, 2, 12])
        var1, rs1, var2, rs2 = (stat[:, i + 4:i + 5] for i in range(4))
        mv1, mv2 = sb("mv1", [P, 2]), sb("mv2", [P, 2])

        names = """x_in powers_ready q_ready term_ready tok_done hi_done lo_done trans_done htok_ready hh_free
                 var1_ready rs1_ready  qk_done qk_evac v_done vt_ready vb_ready qk_written qk_in
                 kb_ready qb_ready s_done sub_done exp_done et_ready o_done ot_ready ott_done csum_done
                 c_ready hi2_done lo2_done var2_ready h2b_ready f0_done f1_done y0_done y_ready y_out
                 cls_out filled dve_passed sp_passed dve_chain act_chain pool_chain""".split()
        s = {n: sem(n) for n in names}
        LAST = GROUPS - 1

        def steps(eng, step, chain=None, per_pass=0):
            step(0, 0, False, True, True)
            step(1, 1, True, True, True)
            with eng.Fori(0, (LAST - 2) // 2) as i:
                if chain:
                    chain.enter(i, per_pass)
                for u in range(2):
                    step(2 * i + (2 + u), u, True, True, True)
            if chain:
                chain.leave((LAST - 2) // 2)
            step(LAST, LAST % 2, True, True, False)
            step(GROUPS, GROUPS % 2, True, False, False)


        with nc.Block() as block:
            @block.sync
            def _(sp):
                def wait(name, count):
                    sp.wait_ge(s[name], count)
                    sp.sem_inc(s["sp_passed"])

                def step(j, u, back, front, ahead):
                    if ahead:
                        if back:
                            wait("powers_ready", j)
                            wait("term_ready", j)
                        for half_ in range(2):
                            sp.dma_start(xc[N * half_:N * half_ + N, :, :], x[:, :, bass.ds(j * (R * C), R * C)]).then_inc(s["x_in"], 16)
                    if front:
                        wait("qk_evac", j + 1)
                        if not isinstance(j, int) or j >= 2:
                            wait("qk_in", 16 * (j - 1))
                        sp.dma_start(scratch[u].rearrange("i g t d -> t (i g) d"),
                                     qk[:, :].rearrange("p (i d) -> p i d", d=D)).then_inc(s["qk_written"], 16)
                        wait("qk_written", 16 * (j + 1))
                        if back:
                            wait("qb_ready", j)
                            wait("kb_ready", j)
                        sp.dma_start(qkc[:, :, :, :].rearrange("p i b d -> p i (b d)"),
                                     scratch[u].rearrange("i g (rs b) d -> (g rs) i (b d)", b=B)).then_inc(s["qk_in"], 16)
                    if back:
                        wait("y_ready", j)
                        if isinstance(j, int) and j == 1:
                            sp.dma_start(out[:, 0, :], yo[0:C, :]).then_inc(s["cls_out"], 16)
                        else:
                            for r in range(R):
                                sp.dma_start(out[:, bass.ds((j - 2) * R + (1 + r), 1), :].rearrange("c o n -> c (o n)"),
                                             yo[C * r:C * r + C, :]).then_inc(s["y_out"], 16)

                steps(sp, step)
                sp.wait_ge(s["cls_out"], 16)
                sp.wait_ge(s["y_out"], 64 * LAST)

            @block.gpsimd
            def _(pool):
                g = nc.gpsimd
                link = Chain(pool, s["pool_chain"])
                g.tensor_copy(VB[:, :, :, G], mask_v.unsqueeze(1).to_broadcast([P, B * S, R])).then_inc(s["filled"], 1)

                def step(j, u, back, front, ahead):
                    if back:
                        pool.wait_ge(s["lo_done"], j)
                        pool.wait_ge(s["hi_done"], j)
                        pool.wait_ge(s["et_ready"], j)
                        g.tensor_tensor(E[:, :], hh[1 - u][:, :, :].bitcast(F32).rearrange("p k n -> p (k n)"),
                                        hl[1 - u][:, :, :].bitcast(F32).rearrange("p k n -> p (k n)"), ALU.add).then_inc(s["csum_done"], 1)
                    if ahead:
                        if back:
                            pool.wait_ge(s["tok_done"], j)
                        p4 = bass.ds(j * R, R)
                        big = lambda at: tab[:, p4, at:at + 8].unsqueeze(3).to_broadcast([P, R, 8, 16])
                        low = lambda at: tab[:, p4, at:at + 16].unsqueeze(2).to_broadcast([P, R, 8, 16])
                        link(g.tensor_tensor(qm[:, :, :, :], big(T_AR), low(T_B1), ALU.mult))
                        link(g.tensor_tensor(qt[:, :, :, :], big(T_AI), low(T_B2), ALU.mult))
                        g.tensor_tensor(qm[:, :, :, :], qm[:, :, :, :], qt[:, :, :, :], ALU.add).then_inc(s["q_ready"], 1)
                        pool.wait_ge(s["q_ready"], j + 1)
                    if front:
                        pool.wait_ge(s["var1_ready"], j + 1)
                        g.tensor_tensor(rs1, var1, half[:, :], ALU.pow).then_inc(s["rs1_ready"], 1)
                    if ahead:
                        pool.wait_ge(s["x_in"], 32 * (j + 1))
                        if back:
                            pool.wait_ge(s["powers_ready"], j)
                        g.tensor_tensor(pt[:, :, :, :], xi.unsqueeze(2).to_broadcast([P, R, K, C]),
                                        u2[:, p4, :].unsqueeze(3).to_broadcast([P, R, K, C]), ALU.mult).then_inc(s["term_ready"], 1)
                    if back:
                        pool.wait_ge(s["var2_ready"], j)
                        link(g.tensor_tensor(rs2, var2, half[:, :], ALU.pow))
                        t = htok[1 - u][:, :, :].rearrange("p k a -> p (k a)")
                        g.tensor_tensor(t, t, ffn_bias[:, :], ALU.add).then_inc(s["h2b_ready"], 1)
                    if front:
                        pool.wait_ge(s["qk_in"], 16 * (j + 1))
                        if back:
                            pool.wait_ge(s["s_done"], j)
                        g.tensor_tensor(QA[:, :, :, :], qkc[:, 0, :, :].unsqueeze(2).to_broadcast([P, B, R, D]),
                                        mask_q.unsqueeze(1).unsqueeze(3).to_broadcast([P, B, R, D]), ALU.mult).then_inc(s["qb_ready"], 1)

                steps(pool, step, link, 2 * 3)

            @block.scalar
            def _(act):
                a_ = nc.scalar
                link = Chain(act, s["act_chain"])

                def h_hi(n, u):
                    act.wait_ge(s["tok_done"], n)
                    if not isinstance(n, int) or n >= 2:
                        act.wait_ge(s["hh_free"], n - 1)
                    a_.activation(hh[u][:, :, :].rearrange("p k (r c) -> p r k c", r=R),
                                  T[:, :].rearrange("p (r k c) -> p r k c", r=R, k=K), ACT.Copy).then_inc(s["hi_done"], 1)

                def step(j, u, back, front, ahead):
                    if front:
                        if not back:
                            a_.activation(hh[u][:, :, :], clst[:, :].unsqueeze(2).to_broadcast([P, K, P]), ACT.Copy).then_inc(s["hi_done"], 1)
                        act.wait_ge(s["trans_done"], j + 1)
                        if not isinstance(j, int) or j >= 2:
                            act.wait_ge(s["y_ready"], j - 1)
                        a_.activation(htok[u][:, :, :].rearrange("p k a -> p (k a)"), HT[:, :], ACT.Copy).then_inc(s["htok_ready"], 1)
                    if back:
                        act.wait_ge(s["c_ready"], j)
                        act.wait_ge(s["v_done"], j)
                        a_.activation(hh[1 - u][:, :, :].rearrange("p k n -> p (k n)"), E[:, :], ACT.Copy).then_inc(s["hi2_done"], 1)
                    if front:
                        act.wait_ge(s["vt_ready"], j + 1)
                        act.wait_ge(s["filled"], 1)
                        if back:
                            act.wait_ge(s["o_done"], j)
                        for r in range(R):
                            m = a_.activation(VB[:, :, r, 0:G], vt[:, :, :].rearrange("p g n -> p n g"), ACT.Copy, scale=mask_v[:, r:r + 1])
                            if r < R - 1:
                                link(m)
                        m.then_inc(s["vb_ready"], 1)
                        act.wait_ge(s["qk_in"], 16 * (j + 1))
                        if back:
                            act.wait_ge(s["s_done"], j)
                        for q in range(S):
                            m = a_.activation(KB[:, :, q, :], qkc[:, 1, :, :], ACT.Copy, scale=mask_k[:, q:q + 1])
                            if q < S - 1:
                                link(m)
                        m.then_inc(s["kb_ready"], 1)
                        act.wait_ge(s["sub_done"], j + 1)
                        a_.activation(E[:, :], E[:, :], ACT.Exp, scale=float(D ** -0.5)).then_inc(s["exp_done"], 1)
                    if ahead:
                        h_hi(j + 1, 1 - u)

                steps(act, step, link, 2 * 6)

            @block.tensor
            def _(pe):
                mm = nc.tensor.matmul

                def triple(dst, left, right, hi, lo, cols, stop_at=None):
                    for k in range(K):
                        for n, (a, w) in enumerate(((hi, left), (lo, left), (hi, right))):
                            m = mm(dst, a(k), w[:, k, cols], start=(k == 0 and n == 0), stop=(k == K - 1 and n == 2))
                    return m

                def h_transposed(n):
                    pe.wait_ge(s["powers_ready"], n)
                    pe.wait_ge(s["q_ready"], n)
                    pe.wait_ge(s["sub_done"], n)
                    for r in range(R):
                        m = mm(T[:, 256 * r:256 * r + 256], qm[:, r, :, :].rearrange("p a b -> p (a b)"),
                               pm[:, r, :, :].rearrange("p k c -> p (k c)"), start=True, stop=True)
                    m.then_inc(s["tok_done"], 1)

                def step(j, u, back, front, ahead):
                    late = not isinstance(j, int) or j >= 2
                    if back:
                        pe.wait_ge(s["et_ready"], j)
                        pe.wait_ge(s["vb_ready"], j)
                        if late:
                            pe.wait_ge(s["y0_done"], j - 1)
                        for n in range(B * S):
                            b, q = n // S, n % S
                            m = mm(O[32 * q:32 * q + 32, b, :, :].rearrange("p r g -> p (r g)"),
                                   ET[:, n, :], VB[:, B * q + b, :, :].rearrange("p r g -> p (r g)"), start=True, stop=True)
                        m.then_inc(s["o_done"], 1)
                    if front:
                        pe.wait_ge(s["hi_done"], j + 1)
                        pe.wait_ge(s["lo_done"], j + 1)
                        if back:
                            pe.wait_ge(s["htok_ready"], j)
                        for k in range(K):
                            for n, a in enumerate((hh[u], hl[u])):
                                m = mm(HT[:, P * k:P * k + P], a[:, k, :], identr[:, :], start=(n == 0), stop=(n == 1))
                        m.then_inc(s["trans_done"], 1)
                    if back:
                        pe.wait_ge(s["ot_ready"], j)
                        if late:
                            pe.wait_ge(s["y_ready"], j - 1)
                        mm(OTOK[:, :], perm, ot[:, :], start=True, stop=True)
                        for q in range(2):
                            m = mm(OT[:, q, :], ot[:, P * q:P * q + P], perm, start=True, stop=True)
                        m.then_inc(s["ott_done"], 1)
                    if front:
                        plain = [lambda k, t=t: t[:, k, :] for t in (hh[u], hl[u])]
                        if back:
                            pe.wait_ge(s["qk_evac"], j)
                        triple(Q[:, 0:QK], wh, wl, *plain, slice(0, QK)).then_inc(s["qk_done"], 1)
                        if back:
                            pe.wait_ge(s["vt_ready"], j)
                        triple(Q[:, QK:QKV], wh, wl, *plain, slice(QK, QKV)).then_inc(s["v_done"], 1)
                    if back:
                        pe.wait_ge(s["hi2_done"], j)
                        pe.wait_ge(s["lo2_done"], j)
                        turned = [lambda k, t=t: t[:, k, :] for t in (hh[1 - u], hl[1 - u])]
                        triple(F[:, 0:512], fh, fl, *turned, slice(0, 512)).then_inc(s["f0_done"], 1)
                    if front:
                        pe.wait_ge(s["qb_ready"], j + 1)
                        pe.wait_ge(s["kb_ready"], j + 1)
                        for b in range(B):
                            m = mm(T[:, P * b:P * b + P], QA[:, b, :, :].rearrange("p r d -> p (r d)"),
                                   KB[:, b, :, :].rearrange("p s e -> p (s e)"), start=True, stop=True)
                        m.then_inc(s["s_done"], 1)
                    if back:
                        pe.wait_ge(s["var2_ready"], j)
                        pe.wait_ge(s["c_ready"], j)
                        for k in range(K):
                            for n, w in enumerate((fh, fl)):
                                m = mm(F[:, 512:1024], hh[1 - u][:, k, :], w[:, k, 512:1024], start=(k == 0 and n == 0), stop=False)
                        m.then_inc(s["hh_free"], 1)
                    if ahead:
                        h_transposed(j + 1)
                    if back:
                        for k in range(K):
                            m = mm(F[:, 512:1024], hl[1 - u][:, k, :], fh[:, k, 512:1024], start=False, stop=(k == K - 1))
                        m.then_inc(s["f1_done"], 1)

                steps(pe, step)

            @block.vector
            def _(dve):
                v = nc.vector
                link = Chain(dve, s["dve_chain"])
                tt = lambda o, a, b, op: link(v.tensor_tensor(o, a, b, op))

                def signal(ins, name, count):
                    ins.then_inc(s[name], 1)
                    dve.wait_ge(s[name], count)

                def variance(t, stats, mv, var, name, count):
                    for n in range(2):
                        link(v.bn_stats(stats[:, 6 * n:6 * n + 6], t[:, 4 * n:4 * n + 4, :].rearrange("p k a -> p (k a)")))
                    dve.sem_inc(s["dve_passed"])
                    link(v.bn_aggr(mv[:, :], stats))
                    signal(v.tensor_scalar(var, mv[:, 1:2], EPS, None, ALU.add), name, count)

                def h_lo(n, u):
                    dve.wait_ge(s["tok_done"], n)
                    dve.wait_ge(s["hi_done"], n + 1)
                    if not isinstance(n, int) or n >= 2:
                        dve.wait_ge(s["f1_done"], n - 1)
                    spread = lambda t: t[:, :, :].rearrange("p k (r c) -> p r k c", r=R)
                    signal(v.tensor_tensor(spread(hl[u]), T[:, :].rearrange("p (r k c) -> p r k c", r=R, k=K),
                                           spread(hh[u]).bitcast(F32), ALU.subtract), "lo_done", n + 1)

                def step(j, u, back, front, ahead):
                    late = not isinstance(j, int) or j >= 2
                    if front and not back:
                        dve.wait_ge(s["hi_done"], 1)
                        signal(v.tensor_tensor(hl[u][:, :, :], clst[:, :].unsqueeze(2).to_broadcast([P, K, P]),
                                               hh[u][:, :, :].bitcast(F32), ALU.subtract), "lo_done", 1)
                    if back:
                        dve.wait_ge(s["o_done"], j)
                        link(v.reciprocal(rden[:, :].rearrange("p (b r) -> p b r", b=B), O[:, :, :, G]))
                        flat = F[:, 0:B * R * GV].rearrange("p (n g) -> p g n", g=GV)[:, 0:G, :]
                        tt(on[:, :, :], flat, rden[:, :].unsqueeze(1).to_broadcast([P, G, 32]), ALU.mult)
                        if late:
                            dve.wait_ge(s["ott_done"], j - 1)
                        signal(v.transpose(ot[:, :].rearrange("p (q d gh) -> p gh q d", q=2, gh=4),
                                           on[:, :, :].rearrange("p (gh q) n -> p gh q n", q=2)), "ot_ready", j)
                        dve.wait_ge(s["ott_done"], j)
                        dve.wait_ge(s["csum_done"], j)
                        c = E[:, :].rearrange("p (q m n) -> p q m n", q=2, m=J)
                        signal(v.tensor_tensor(c, c, OT[:, :, :].unsqueeze(2).to_broadcast([P, 2, J, P]), ALU.add), "c_ready", j)
                    if front:
                        dve.wait_ge(s["htok_ready"], j + 1)
                        if back:
                            dve.wait_ge(s["rs1_ready"], j)
                        variance(htok[u], bn[:, 0, :], mv1, var1, "var1_ready", j + 1)
                    if back:
                        dve.wait_ge(s["hi2_done"], j)
                        signal(v.tensor_tensor(hl[1 - u][:, :, :].rearrange("p k n -> p (k n)"), E[:, :],
                                               hh[1 - u][:, :, :].bitcast(F32).rearrange("p k n -> p (k n)"), ALU.subtract), "lo2_done", j)
                        t = htok[1 - u]
                        c = t[:, :, :].rearrange("p (q m) a -> p q m a", q=2)
                        tt(c, c, OTOK.rearrange("p (q a) -> p q a", q=2).unsqueeze(2).to_broadcast([P, 2, J, P]), ALU.add)
                    if front:
                        dve.wait_ge(s["rs1_ready"], j + 1)
                        dve.wait_ge(s["qk_done"], j + 1)
                        if back:
                            dve.wait_ge(s["qk_written"], 16 * j)
                        signal(v.scalar_tensor_tensor(qk[:, :], Q[:, 0:QK], rs1, qkv_bias[:, 0:QK], ALU.mult, ALU.add), "qk_evac", j + 1)
                    if back:
                        if late:
                            dve.wait_ge(s["h2b_ready"], j - 1)
                        variance(t, bn[:, 1, :], mv2, var2, "var2_ready", j)
                    if front:
                        dve.wait_ge(s["v_done"], j + 1)
                        link(v.scalar_tensor_tensor(vs[:, :], Q[:, QK:QKV], rs1, qkv_bias[:, QK:QKV], ALU.mult, ALU.add))
                        if back:
                            dve.wait_ge(s["vb_ready"], j)
                        signal(v.transpose(vt[:, :, :].rearrange("p g n -> p (g n)"), vs[:, :]), "vt_ready", j + 1)
                    if ahead:
                        dve.wait_ge(s["x_in"], 32 * (j + 1))
                        if back:
                            dve.wait_ge(s["tok_done"], j)
                        tt(pm[:, :, :, :], xr.unsqueeze(2).to_broadcast([P, R, K, C]),
                           u1[:, bass.ds(j * R, R), :].unsqueeze(3).to_broadcast([P, R, K, C]), ALU.mult)
                        dve.wait_ge(s["term_ready"], j + 1)
                        signal(v.tensor_tensor(pm[:, :, :, :], pm[:, :, :, :], pt[:, :, :, :], ALU.add), "powers_ready", j + 1)

                    def rows(n):
                        at = slice(512 * n, 512 * n + 512)
                        return v.scalar_tensor_tensor(
                            yo[:, at].rearrange("p (a k) -> p a k", k=K), F[:, at].rearrange("p (a k) -> p a k", k=K), rs2,
                            htok[1 - u][:, :, 64 * n:64 * n + 64].rearrange("p k a -> p a k"), ALU.mult, ALU.add)

                    if back:
                        dve.wait_ge(s["f0_done"], j)
                        dve.wait_ge(s["h2b_ready"], j)
                        if late:
                            dve.wait_ge(s["cls_out"], 16)
                        if not isinstance(j, int) or j >= 3:
                            dve.wait_ge(s["y_out"], 64 * (j - 2))
                        signal(rows(0), "y0_done", j)
                    if front:
                        dve.wait_ge(s["s_done"], j + 1)
                        sc = T[:, :].rearrange("p (n e) -> p n e", e=D)
                        link(v.tensor_reduce(mx[:, :], sc, AX_X, ALU.max))
                        if back:
                            dve.wait_ge(s["lo2_done"], j)
                        signal(v.tensor_tensor(E[:, :].rearrange("p (n e) -> p n e", e=D), sc,
                                               mx[:, :].unsqueeze(2).to_broadcast([P, B * S, D]), ALU.subtract), "sub_done", j + 1)
                        dve.wait_ge(s["exp_done"], j + 1)
                        signal(v.transpose(ET[:, :, :].rearrange("p n d -> p (n d)"), E[:, :]), "et_ready", j + 1)
                    if ahead:
                        h_lo(j + 1, 1 - u)
                    if back:
                        dve.wait_ge(s["f1_done"], j)
                        signal(rows(1), "y_ready", j)

                steps(dve, step, link, 2 * (2 + 3 + 1 + 3 + 1 + 1 + 1))


def kernel(x, cls_tok, L0_tok_A_abslog, L0_tok_A_phase, L0_attn_Wq, L0_attn_bq, L0_attn_Wk, L0_attn_bk,
           L0_attn_Wv, L0_attn_bv, L0_ffn_W, L0_ffn_bias, L0_ffn_A, L0_ffn_Bf, L0_ffn_coeffs, L0_ffn_scales):
    import concourse.bacc as bacc
    from concourse.bass_utils import run_bass_kernel_spmd

    def by_group(w):
        w = np.asarray(w)
        w = w.reshape(*w.shape[:-1], G, w.shape[-1] // G)
        w = np.moveaxis(w, -2, -3)
        return w.reshape(*w.shape[:-3], -1)

    chunked = lambda w: np.moveaxis(w.reshape(*w.shape[:-1], P, K), -1, -2).reshape(*w.shape[:-1], L)
    arrays = {
        "x": np.ascontiguousarray(np.transpose(np.asarray(x), (2, 3, 1, 0)).reshape(N, 2, H * C)),
        "modes": np.stack([np.asarray(L0_tok_A_phase).T, np.asarray(L0_tok_A_abslog).T], 1),
        "cls": np.ascontiguousarray(np.asarray(cls_tok).reshape(L)),
        "wq": np.ascontiguousarray(by_group(L0_attn_Wq)),
        "wkv": np.ascontiguousarray(np.concatenate([by_group(L0_attn_Wk), by_group(L0_attn_Wv)], -1)),
        "bq": np.ascontiguousarray(by_group(L0_attn_bq)),
        "bkv": np.ascontiguousarray(np.concatenate([by_group(L0_attn_bk), by_group(L0_attn_bv)], -1)),
        "wt": np.ascontiguousarray(np.asarray(L0_ffn_W).T),
        "fbias": np.ascontiguousarray(chunked(np.asarray(L0_ffn_bias))),
        "fa": np.ascontiguousarray(chunked(np.asarray(L0_ffn_A).reshape(ER, L))),
        "fb": np.ascontiguousarray(np.transpose(np.asarray(L0_ffn_Bf), (0, 2, 1)).reshape(ER, L)),
        "gates": np.ascontiguousarray(np.concatenate([np.repeat(np.asarray(a), 16).reshape(2, P)
                                       for a in (L0_ffn_coeffs, L0_ffn_scales)]).T),
        "const": constants(),
        "maps": part_maps(),
    }
    nc = bacc.Bacc("TRN2", target_bir_lowering=False, num_devices=1)
    ins = [nc.dram_tensor(f"in_{n}", a.shape, mybir.dt.from_np(a.dtype), kind="ExternalInput").ap()
           for n, a in arrays.items()]
    y = nc.dram_tensor("out_rows", (C, H + 1, L), F32, kind="ExternalOutput").ap()
    tower(nc, *ins, y)
    r = run_bass_kernel_spmd(nc, [{f"in_{n}": a for n, a in arrays.items()}], core_ids=[0])
    return r.results[0]["out_rows"]
```

```python
from contextlib import ExitStack

import concourse.bass as bass
import numpy as np
from concourse import mybir

ALU = mybir.AluOpType
ACT = mybir.ActivationFunctionType
AX_X = mybir.AxisListType.X
F32 = mybir.dt.float32
F32R = mybir.dt.float32r

P = 128
C, H, N, L = 32, 64, 64, 1024
K = L // P
R, S, B = 4, 4, 8
D, G, J = 32, 8, 4
QK = 2 * G * D
QKV = 3 * G * D
ER = 256
GROUPS = 1 + H // R
GV = G + 1
EPS = 1e-5

T_B1, T_B2, T_AR, T_AI, T_ALL = 0, 16, 32, 40, 48
Z_B, Z_A, Z_V, Z_ALL = 0, 16, 24, 32
HALVES = 2
RING = 4
LORA_BANKS = 3
KSUM_POOL = K - 2
F_LO_POOL = 3
W_PARTS = ["keys and values, 0", "keys and values, 1", "queries"]
WEIGHT_ORDER = [0, 1, 2, 3, 4, *W_PARTS, 5, 6]

F1_FIRST, F1_SECOND, V_FIRST = 2, 16, 14

C_ID, C_PERM, C_MV, C_MQ, C_MK, C_POW = 0, 128, 256, 260, 264, 268
C_OFF = C_POW + Z_ALL
C_ALL = C_OFF + 1
ROUND = 1.5 * 2.0 ** 23
INV_HI = float(np.floor(2.0 ** 14 / (2 * np.pi)) / 2.0 ** 14)
INV_LO = float(1 / (2 * np.pi) - INV_HI)
TWO_PI = 6.283185


def constants():
    c = np.zeros((P, C_ALL), np.float32)
    p = np.arange(P)
    c[p, C_ID + p] = 1
    r, s, b = p // 32, p % 32 // 8, p % 8
    c[32 * s + 4 * b + r, C_PERM + p] = 1
    c[p, C_MV + p // 32] = 1
    c[p, C_MQ + p % 16 // 4] = 1
    c[p, C_MK + p % 4] = 1
    c[:, C_POW + Z_B:C_POW + Z_A] = 8 * np.arange(16)
    c[:, C_POW + Z_A:C_POW + Z_V] = 128 * np.arange(8)
    c[:, C_POW + Z_V:C_POW + Z_ALL] = np.arange(8)
    c[:N, C_OFF] = 0.25
    return c


def part_maps():
    m = np.zeros((P, 5, P), np.float32)
    n = np.arange(N)
    for i, ((top, top_sign), (low, low_sign)) in enumerate([
            ((1, -1), (0, 1)), ((0, 1), (0, 1)), ((1, 1), (1, 1)), ((0, 1), (1, -1)), ((1, -1), (0, -1))]):
        m[N * top + n, i, n] = top_sign
        m[N * low + n, i, N + n] = low_sign
    return m


class Chain:

    def __init__(self, eng, sem):
        self.eng, self.sem, self.n, self.past = eng, sem, 0, 0

    def __call__(self, ins):
        self.n += 1
        ins.then_inc(self.sem, 1)
        self.eng.wait_ge(self.sem, self.past + self.n)

    def enter(self, i, per_pass):
        self.past, self.at, self.per_pass = i * per_pass, self.n, per_pass

    def leave(self, passes):
        assert self.n - self.at == self.per_pass, (self.n - self.at, self.per_pass)
        self.n, self.past = self.at + passes * self.per_pass, 0


def tower(nc, x, modes, cls, wq, wkv, bq, bkv, wt, fbias, fa, fb, gates, const, maps, out):
    ctx = ExitStack()
    with ctx:
        sem = lambda name: ctx.enter_context(nc.semaphore(name))

        def sb(name, shape, dt=F32, into=ctx):
            return into.enter_context(nc.sbuf_tensor(name, shape, dt))

        with ExitStack() as under_wh:
            ring = sb("ring", [P, RING, L], F32, under_wh)
            part = sb("part", [P, 5, P], F32, under_wh)
            bq_raw = sb("bq_raw", [P, L], F32, under_wh)
        wh = sb("wh", [P, K, QKV], F32R)
        with ExitStack() as under_wl:
            wsum = sb("wsum", [P, K, QKV], F32, under_wl)
        wl = sb("wl", [P, K, QKV], F32R)
        fh = sb("fh", [P, K, L], F32R)
        with ExitStack() as under_fl:
            stage = sb("stage", [P, K, L], F32, under_fl)
        fl = sb("fl", [P, K, L], F32R)
        tab = sb("tab", [P, H, T_ALL])
        u1, u2 = sb("u1", [P, H, 8]), sb("u2", [P, H, 8])
        cst = sb("cst", [P, C_ALL])
        qkv_bias, ffn_bias = sb("qkv_bias", [P, QKV]), sb("ffn_bias", [P, L])
        clst = sb("clst", [P, K])
        stat = sb("stat", [P, 16])
        half = sb("half", [P, 1])
        ident = cst[:, C_ID:C_ID + P]
        perm = cst[:, C_PERM:C_PERM + P]
        mask_v = cst[:, C_MV:C_MV + R]
        mask_q = cst[:, C_MQ:C_MQ + R]
        mask_k = cst[:, C_MK:C_MK + S]

        T = ctx.enter_context(nc.psum_tensor("T", [P, L], F32))
        Q = ctx.enter_context(nc.psum_tensor("Q", [P, L], F32))
        HT = ctx.enter_context(nc.psum_tensor("HT", [P, L], F32))
        F = ctx.enter_context(nc.psum_tensor("F", [P, L], F32))
        O = F[:, 0:B * R * GV].rearrange("p (b r g) -> p b r g", b=B, r=R)
        OTOK = T[:, 0:256]
        OT = F[:, 768:1024].rearrange("p (q n) -> p q n", q=2)

        scratch = [nc.dram_tensor(f"qk_scratch{i}", (2, G, P, D), F32, kind="Internal").ap()
                   for i in range(2)]

        with ExitStack() as early:
            lora_a, lora_b = sb("lora_a", [P, 2, L], F32, early), sb("lora_b", [P, 2, L], F32, early)
            arg, turns, mag, rest = (sb(n, [P, H, Z_ALL], F32, early) for n in ("arg", "turns", "mag", "rest"))
            mode, small = sb("mode", [P, 2, H], F32, early), sb("small", [P, 8, H], F32, early)
            phr = sb("phr", [P, 2, H], F32R, early)
            ksum = sb("ksum", [P, 2, L], F32, early)
            z = sb("z", [P, 2, H], F32, early)
            ksum_hi, ksum_lo = sb("ksum_hi", [P, L], F32R, early), sb("ksum_lo", [P, L], F32R, early)
            ones, minus = sb("ones", [P, P], F32, early), sb("minus", [P, P], F32R, early)
            gate = sb("gate", [P, 8], F32, early)
            ph, al = mode[:, 0, :], mode[:, 1, :]
            w_sums = turns[:, :, :].rearrange("p h n -> p (h n)")
            kv_sum, q_sum = w_sums[:, 0:2 * G * D], w_sums[:, 2 * G * D:3 * G * D]
            vv = mag[:, :, :].rearrange("p h n -> p (h n)")[:, 0:2 * 8 * H].rearrange("p (i h b) -> p i h b", i=2, h=H)

            modes_in, a_in, b_in, small_in = sem("modes_in"), sem("a_in"), sem("b_in"), sem("small_in")
            wt_in = [sem(f"wt_in{i}") for i in range(2)]
            wkv_in = sem("wkv_in")
            wq_in = [sem(f"wq_in{i}") for i in range(RING)]
            dve0, pool0 = sem("dve_setup"), sem("pool_setup")
            phases_ready, rest_ready, args_ready, mags_ready = (
                sem(n) for n in ("phases_ready", "rest_ready", "args_ready", "mags_ready"))
            sines_done, mags_done, base_ready = sem("sines_done"), sem("mags_done"), sem("base_ready")
            mapped, v_copied, z_copied, swapped_copied, parts_copied, f_ready = (
                sem(n) for n in ("mapped", "v_copied", "z_copied", "swapped_copied", "parts_copied", "f_ready"))
            kv_summed, q_summed = sem("kv_summed"), sem("q_summed")
            lora_scaled, ones_ready, rest_summed, ksum_ready, ksum_hi_ready, ksum_split = (
                sem(n) for n in ("lora_scaled", "ones_ready", "rest_summed", "ksum_ready", "ksum_hi_ready", "ksum_split"))
            lora_done, merged = sem("lora_done"), sem("merged")
            wq_summed, kv_mean, q_mean, centred, w_hi_done = (
                sem(n) for n in ("wq_summed", "kv_mean", "q_mean", "centred", "w_hi_done"))
            banks = [T, Q, HT]
            GD = G * D
            halves = [slice(H // HALVES * i, H // HALVES * (i + 1)) for i in range(HALVES)]
            w_parts = [(slice(0, K // 2), slice(GD, QKV)), (slice(K // 2, K), slice(GD, QKV)), (slice(0, K), slice(0, GD))]

            with nc.Block() as block:
                @block.sync
                def _(sp):
                    for i in range(2):
                        sp.dma_start(mode[N * i:N * i + N, :, :], modes).then_inc(modes_in, 16)
                    sp.dma_start(cst[:, :], const).then_inc(modes_in, 16)
                    sp.dma_start(gate[:, 0:4], gates).then_inc(a_in, 16)
                    sp.dma_start(lora_a[:, :, :], fa.rearrange("(q p) n -> p q n", p=P)).then_inc(a_in, 16)
                    sp.dma_start(lora_b[:, :, :], fb.rearrange("(q p) n -> p q n", p=P)).then_inc(b_in, 16)
                    for i in range(2):
                        ks = slice(K // 2 * i, K // 2 * (i + 1))
                        sp.dma_start(stage[:, ks, :], wt.rearrange("(a k) n -> a k n", k=K)[:, ks, :]).then_inc(wt_in[i], 16)
                    sp.dma_start(part[:, :, :], maps).then_inc(small_in, 16)
                    sp.dma_start(wsum[:, :, GD:], wkv.rearrange("(a k) n -> a k n", k=K)).then_inc(wkv_in, 16)
                    for k in range(K):
                        if k >= RING:
                            sp.wait_ge(wq_summed, k - RING + 1)
                        sp.dma_start(ring[:, k % RING, :], wq.rearrange("(a k) n -> a k n", k=K)[:, k, :]).then_inc(wq_in[k % RING], 16)
                    sp.dma_start(clst[:, :], cls.rearrange("(a k) -> a k", k=K)).then_inc(small_in, 16)
                    sp.dma_start(bq_raw[:, :], bq.partition_broadcast(P)).then_inc(small_in, 16)
                    sp.dma_start(qkv_bias[:, GD:], bkv.partition_broadcast(P)).then_inc(small_in, 16)
                    sp.dma_start(ffn_bias[:, :], fbias.partition_broadcast(P)).then_inc(small_in, 16)

                @block.gpsimd
                def _(pool):
                    g = nc.gpsimd
                    link = Chain(pool, pool0)
                    pool.wait_ge(modes_in, 3 * 16)
                    power = cst[:, C_POW:C_POW + Z_ALL].unsqueeze(1).to_broadcast([P, H // HALVES, Z_ALL])
                    wide = lambda a, hs: a[:, hs].unsqueeze(2).to_broadcast([P, H // HALVES, Z_ALL])
                    pool.wait_ge(phases_ready, 1)
                    for hs in halves:
                        g.tensor_tensor(rest[:, hs, :], wide(small[:, 1, :], hs), power, ALU.mult).then_inc(rest_ready, 1)
                    for hs in halves:
                        g.tensor_tensor(mag[:, hs, :], wide(al, hs), power, ALU.mult).then_inc(mags_ready, 1)
                    pool.wait_ge(wt_in[0], 16)
                    link(g.tensor_tensor(ksum[:, 0, :], stage[:, 0, :], stage[:, 1, :], ALU.add))
                    for k in range(2, KSUM_POOL):
                        if k == K // 2:
                            pool.wait_ge(wt_in[1], 16)
                        link(g.tensor_tensor(ksum[:, 0, :], ksum[:, 0, :], stage[:, k, :], ALU.add))
                    pool.wait_ge(rest_summed, 1)
                    g.tensor_tensor(ksum[:, 0, :], ksum[:, 0, :], ksum[:, 1, :], ALU.add).then_inc(ksum_ready, 1)
                    pool.wait_ge(ksum_hi_ready, 1)
                    g.tensor_tensor(ksum_lo[:, :], ksum[:, 0, :], ksum_hi[:, :].bitcast(F32), ALU.subtract).then_inc(ksum_split, 1)
                    pool.wait_ge(wkv_in, 16)
                    pool.wait_ge(args_ready, HALVES)
                    link(g.tensor_tensor(kv_sum, wsum[:, 0, GD:], wsum[:, 1, GD:], ALU.add))
                    for k in range(2, K):
                        m = g.tensor_tensor(kv_sum, kv_sum, wsum[:, k, GD:], ALU.add)
                        if k < K - 1:
                            link(m)
                    m.then_inc(kv_summed, 1)
                    pool.wait_ge(v_copied, 1)
                    pool.wait_ge(f_ready, 1)
                    f1, f2 = (small[:, i, :].unsqueeze(2).to_broadcast([P, H, 8]) for i in (5, 6))
                    v1, v2 = vv[:, 0, :, :], vv[:, 1, :, :]
                    tmp = rest[:, :, 0:8]
                    for u, (a, b), op in ((u1, (v1, v2), ALU.add), (u2, (v2, v1), ALU.subtract)):
                        link(g.tensor_tensor(u[:, :, :], f1, a, ALU.mult))
                        link(g.tensor_tensor(tmp, f2, b, ALU.mult))
                        link(g.tensor_tensor(u[:, :, :], u[:, :, :], tmp, op))
                    pool.wait_ge(wq_summed, 2)
                    link(g.tensor_tensor(q_sum, wsum[:, 0, 0:GD], wsum[:, 1, 0:GD], ALU.add))
                    for k in range(2, K):
                        pool.wait_ge(wq_summed, k + 1)
                        m = g.tensor_tensor(q_sum, q_sum, wsum[:, k, 0:GD], ALU.add)
                        if k < K - 1:
                            link(m)
                    m.then_inc(q_summed, 1)
                    ks, at = w_parts[0]
                    pool.wait_ge(w_hi_done, 1)
                    link(g.tensor_tensor(wl[:, ks, at], wsum[:, ks, at], wh[:, ks, at].bitcast(F32), ALU.subtract))

                @block.scalar
                def _(act):
                    for i, hs in enumerate(halves):
                        act.wait_ge(mags_ready, i + 1)
                        nc.scalar.activation(mag[:, hs, :], mag[:, hs, :], ACT.Exp).then_inc(mags_done, 1)
                    for i, hs in enumerate(halves):
                        act.wait_ge(args_ready, i + 1)
                        nc.scalar.activation(arg[:, hs, :], arg[:, hs, :], ACT.Sin, scale=TWO_PI).then_inc(sines_done, 1)
                    act.wait_ge(ksum_ready, 1)
                    nc.scalar.activation(ksum_hi[:, :], ksum[:, 0, :], ACT.Copy).then_inc(ksum_hi_ready, 1)
                    act.wait_ge(mags_done, HALVES)
                    act.wait_ge(base_ready, 1)
                    act.wait_ge(mapped, 1)
                    nc.scalar.activation(vv, F[:, :].rearrange("p (i h b) -> p i h b", i=2, h=H), ACT.Copy).then_inc(v_copied, 1)
                    act.wait_ge(mapped, 2)
                    nc.scalar.activation(z[:, :, :], F[:, :].rearrange("p (i n) -> p i n", i=2)[:, :, 0:H], ACT.Copy).then_inc(z_copied, 1)
                    act.wait_ge(mapped, 3)
                    nc.scalar.activation(tab[:, :, T_B2:T_AR], F[:, :].rearrange("p (h b) -> p h b", h=H), ACT.Copy).then_inc(swapped_copied, 1)
                    act.wait_ge(mapped, 4)
                    nc.scalar.activation(tab[:, :, T_AR:].rearrange("p h (i a) -> p i h a", i=2),
                                         F[:, :].rearrange("p (i h a) -> p i h a", i=2, h=H), ACT.Copy).then_inc(parts_copied, 1)
                    for n in WEIGHT_ORDER:
                        if isinstance(n, str):
                            i = W_PARTS.index(n)
                            ks, at = w_parts[i]
                            act.wait_ge(centred, i + 1)
                            act.wait_ge(wq_summed, K + 1)
                            nc.scalar.activation(wh[:, ks, at], wsum[:, ks, at], ACT.Copy).then_inc(w_hi_done, 1)
                        else:
                            act.wait_ge(merged, n + 1)
                            nc.scalar.activation(fh[:, n, :], stage[:, n, :], ACT.Copy)

                @block.tensor
                def _(pe):
                    mm = nc.tensor.matmul

                    def experts(k):
                        for o in range(2):
                            for q in range(2):
                                m = mm(banks[k % LORA_BANKS][:, 512 * o:512 * o + 512], lora_a[:, q, P * k:P * k + P],
                                       lora_b[:, q, 512 * o:512 * o + 512], start=(q == 0), stop=False)

                    def less_mean(k):
                        for o in range(2):
                            for n, t in enumerate((ksum_hi, ksum_lo)):
                                m = mm(banks[k % LORA_BANKS][:, 512 * o:512 * o + 512], minus[:, :], t[:, 512 * o:512 * o + 512],
                                       start=False, stop=(n == 1))
                        m.then_inc(lora_done, 1)

                    def to_parts(which, powers):
                        for o in range(2):
                            src = powers(o)
                            m = mm(F[:, 512 * o:512 * o + int(np.prod(src.shape[1:]))], part[:, which[o], :], src, start=True, stop=True)
                        m.then_inc(mapped, 1)

                    pe.wait_ge(ones_ready, 2)
                    pe.wait_ge(lora_scaled, 2)
                    pe.wait_ge(b_in, 16)
                    for k in range(LORA_BANKS):
                        experts(k)
                    pe.wait_ge(small_in, 16)
                    pe.wait_ge(base_ready, 1)
                    to_parts((3, 4), lambda o: arg[:, :, Z_V:])
                    pe.wait_ge(v_copied, 1)
                    to_parts((1, 2), lambda o: arg[:, :, Z_V + 1])
                    pe.wait_ge(z_copied, 1)
                    to_parts((0, 0), lambda o: tab[:, 32 * o:32 * o + 32, T_B1:T_B2])
                    pe.wait_ge(ksum_hi_ready, 1)
                    pe.wait_ge(ksum_split, 1)
                    less_mean(0)
                    less_mean(1)
                    pe.wait_ge(swapped_copied, 1)
                    to_parts((1, 2), lambda o: arg[:, :, Z_A:Z_V])
                    less_mean(2)
                    for k in range(LORA_BANKS, K):
                        pe.wait_ge(merged, k - LORA_BANKS + 1)
                        experts(k)
                        less_mean(k)
                        if k == LORA_BANKS:
                            pe.wait_ge(parts_copied, 1)
                            pe.wait_ge(kv_summed, 1)
                            mm(F[:, 0:2 * GD], ones[:, :], kv_sum, start=True, stop=True).then_inc(kv_mean, 1)
                        if k == LORA_BANKS + 2:
                            pe.wait_ge(q_summed, 1)
                            mm(F[:, 2 * GD:3 * GD], ones[:, :], q_sum, start=True, stop=True).then_inc(q_mean, 1)

                @block.vector
                def _(dve):
                    v = nc.vector
                    link = Chain(dve, dve0)
                    tt = lambda o, a, b, op: link(v.tensor_tensor(o, a, b, op))
                    sm = lambda i: small[:, i, :]
                    link(v.memset(half[:, :], -0.5))
                    link(v.memset(ones[:, :], -1.0 / L))
                    v.tensor_copy(minus[:, :], ones[:, :]).then_inc(ones_ready, 1)
                    dve.wait_ge(ones_ready, 1)
                    v.memset(ones[:, :], 1.0 / L).then_inc(ones_ready, 1)
                    dve.wait_ge(modes_in, 3 * 16)
                    link(v.tensor_copy(phr[:, 0, :], ph))
                    p_hi = phr[:, 0, :].bitcast(F32)
                    t_hi = phr[:, 1, :].bitcast(F32)
                    tt(sm(0), ph, p_hi, ALU.subtract)
                    link(v.tensor_scalar(sm(1), p_hi, INV_HI, None, ALU.mult))
                    link(v.tensor_copy(phr[:, 1, :], sm(1)))
                    tt(sm(1), sm(1), t_hi, ALU.subtract)
                    link(v.scalar_tensor_tensor(sm(1), p_hi, INV_LO, sm(1), ALU.mult, ALU.add))
                    v.scalar_tensor_tensor(sm(1), sm(0), INV_HI + INV_LO, sm(1), ALU.mult, ALU.add).then_inc(phases_ready, 1)
                    dve.wait_ge(phases_ready, 1)
                    dve.wait_ge(a_in, 2 * 16)
                    tt(gate[:, 0:2], gate[:, 0:2], gate[:, 2:4], ALU.mult)
                    link(v.tensor_reduce(gate[:, 4:6], lora_a[:, :, :], AX_X, ALU.add))
                    link(v.tensor_scalar(gate[:, 4:6], gate[:, 4:6], 1.0 / L, None, ALU.mult))
                    for q in range(2):
                        v.tensor_scalar(lora_a[:, q, :], lora_a[:, q, :], gate[:, 4 + q:5 + q], gate[:, q:q + 1],
                                        ALU.subtract, ALU.mult).then_inc(lora_scaled, 1)
                    off = cst[:, C_OFF:C_OFF + 1]
                    power = cst[:, C_POW:C_POW + Z_ALL].unsqueeze(1).to_broadcast([P, H // HALVES, Z_ALL])
                    for i, hs in enumerate(halves):
                        t, a = turns[:, hs, :], arg[:, hs, :]
                        tt(t, t_hi[:, hs].unsqueeze(2).to_broadcast([P, H // HALVES, Z_ALL]), power, ALU.mult)
                        link(v.tensor_scalar(a, t, ROUND, ROUND, ALU.add, ALU.subtract))
                        tt(t, t, a, ALU.subtract)
                        dve.wait_ge(rest_ready, i + 1)
                        link(v.scalar_tensor_tensor(t, t, off, rest[:, hs, :], ALU.add, ALU.add))
                        link(v.tensor_scalar(a, t, ROUND, ROUND, ALU.add, ALU.subtract))
                        v.tensor_tensor(a, t, a, ALU.subtract).then_inc(args_ready, 1)
                    dve.wait_ge(wt_in[1], 16)
                    v.tensor_tensor(ksum[:, 1, :], stage[:, KSUM_POOL, :], stage[:, K - 1, :], ALU.add).then_inc(rest_summed, 1)
                    for i, hs in enumerate(halves):
                        dve.wait_ge(sines_done, i + 1)
                        dve.wait_ge(mags_done, i + 1)
                        link(v.tensor_tensor(tab[:, hs, T_B1:T_B2], arg[:, hs, Z_B:Z_A], mag[:, hs, Z_B:Z_A], ALU.mult))
                        m = v.tensor_tensor(arg[:, hs, Z_A:], arg[:, hs, Z_A:], mag[:, hs, Z_A:], ALU.mult)
                        if i < HALVES - 1:
                            link(m)
                    m.then_inc(base_ready, 1)

                    def sum_wq(k):
                        dve.wait_ge(wq_in[k % RING], 16 * (k // RING + 1))
                        v.tensor_reduce(wsum[:, k, 0:GD], ring[:, k % RING, :].rearrange("p (n j) -> p n j", j=J),
                                        AX_X, ALU.add).then_inc(wq_summed, 1)

                    def merge(k):
                        dve.wait_ge(lora_done, k + 1)
                        v.tensor_tensor(stage[:, k, :], stage[:, k, :], banks[k % LORA_BANKS][:, :], ALU.add).then_inc(merged, 1)

                    def centre(i):
                        ks, at = w_parts[i]
                        dve.wait_ge(kv_mean if i < 2 else q_mean, 1)
                        mean = F[:, at.start - GD:at.stop - GD] if i < 2 else F[:, 2 * GD:3 * GD]
                        w = wsum[:, ks, at]
                        v.tensor_tensor(w, w, mean.unsqueeze(1).to_broadcast(list(w.shape)), ALU.subtract).then_inc(centred, 1)

                    for k in range(RING):
                        sum_wq(k)
                    link(v.tensor_scalar(sm(2), t_hi, ROUND, ROUND, ALU.add, ALU.subtract))
                    tt(sm(2), t_hi, sm(2), ALU.subtract)
                    tt(sm(2), sm(2), sm(1), ALU.add)
                    link(v.tensor_scalar(sm(3), sm(2), ROUND, ROUND, ALU.add, ALU.subtract))
                    tt(sm(2), sm(2), sm(3), ALU.subtract)
                    link(v.tensor_scalar(sm(2), sm(2), float(2 * np.pi), None, ALU.mult))
                    tt(sm(4), al, al, ALU.mult)
                    tt(sm(5), sm(2), sm(2), ALU.mult)
                    tt(sm(4), sm(4), sm(5), ALU.add)
                    link(v.reciprocal(sm(4), sm(4)))
                    link(v.tensor_scalar(sm(4), sm(4), 2.0, None, ALU.mult))
                    dve.wait_ge(z_copied, 1)
                    im = z[:, 1, :]
                    link(v.tensor_scalar(sm(3), z[:, 0, :], 1.0, None, ALU.subtract))
                    tt(sm(5), sm(3), al, ALU.mult)
                    tt(sm(7), im, sm(2), ALU.mult)
                    tt(sm(5), sm(5), sm(7), ALU.add)
                    tt(sm(5), sm(5), sm(4), ALU.mult)
                    tt(sm(6), im, al, ALU.mult)
                    tt(sm(7), sm(3), sm(2), ALU.mult)
                    tt(sm(6), sm(6), sm(7), ALU.subtract)
                    v.tensor_tensor(sm(6), sm(6), sm(4), ALU.mult).then_inc(f_ready, 1)
                    for k in range(LORA_BANKS):
                        merge(k)
                    for k in range(RING, K):
                        sum_wq(k)
                        if k == RING + 1:
                            merge(3)
                    dve.wait_ge(small_in, 5 * 16)
                    v.tensor_reduce(qkv_bias[:, 0:GD], bq_raw[:, :].rearrange("p (n j) -> p n j", j=J), AX_X, ALU.add).then_inc(wq_summed, 1)
                    merge(4)
                    for i in range(3):
                        centre(i)
                    ks, at = w_parts[1]
                    dve.wait_ge(w_hi_done, 2)
                    link(v.tensor_tensor(wl[:, ks, at], wsum[:, ks, at], wh[:, ks, at].bitcast(F32), ALU.subtract))
                    for k in (5, 6, 7):
                        merge(k)

        hh = [sb(f"hh{i}", [P, K, P], F32R) for i in range(2)]
        hl = [sb(f"hl{i}", [P, K, P], F32R) for i in range(2)]
        hw = [sb(f"hw{i}", [P, K, P]) for i in range(2)]
        xc = sb("xc", [P, 2, R * C])
        xr, xi = (xc[:, i, :].rearrange("p (r c) -> p r c", r=R) for i in range(2))
        pm, pt = sb("pm", [P, R, K, C]), sb("pt", [P, R, K, C])
        qm = sb("qm", [P, R, 8, 16])
        qt = pt[:, :, :, :].rearrange("p r k c -> p (r k c)")[:, 0:R * P].rearrange("p (r a b) -> p r a b", r=R, a=8)
        htok = [sb(f"htok{i}", [P, K, P]) for i in range(2)]
        E = sb("E", [P, L])
        ET = sb("ET", [P, B * S, D])
        QA, KB = sb("QA", [P, B, R, D]), sb("KB", [P, B, S, D])
        qkc = sb("qkc", [P, 2, B, D])
        qk, vt = sb("qk", [P, QK]), sb("vt", [P, G, 32])
        VB = sb("VB", [P, B * S, R, GV])
        on, ot = sb("on", [P, G, 32]), sb("ot", [P, G * D])
        vs = on[:, :, :].rearrange("p g n -> p (g n)")
        mx, rden = sb("mx", [P, B * S]), sb("rden", [P, B * R])
        bn = sb("bn", [P, 2, 12])
        var1, rs1, var2, rs2 = (stat[:, i + 4:i + 5] for i in range(4))
        mv1, mv2 = sb("mv1", [P, 2]), sb("mv2", [P, 2])

        names = """x_in term_ready powers_ready q_ready tok_done hi_done whole_done lo_done trans_done htok_ready
                 var1_ready rs1_ready qk_done qk_evac v_done vt_ready vb_ready qk_written qk_in
                 kb_ready qb_ready s_done sub_done exp_done et_ready o_done ot_ready ott_done otok_done
                 c_ready hi2_done lo2_done otok_read var2_ready h2b_ready f0_done f1_done y0_done y_ready
                 y_out filled last_hi queries_split output_split output_split_pool dve_passed sp_passed dve_chain act_chain pool_chain""".split()
        s = {n: sem(n) for n in names}
        LAST = GROUPS - 1
        k_halves = [slice(0, K // 2), slice(K // 2, K)]
        FIRST, PASSES = 3, (LAST - 4) // 2

        def later(n, m=1):
            return not isinstance(n, int) or n >= m

        def parts(i):
            if not isinstance(i, int):
                return True, True, True
            return i <= LAST, i < LAST, i + 1 < LAST

        def steps(eng, start, step, chain=None, per_pass=0):
            start()
            for i in range(1, FIRST):
                step(i, i % 2)
            with eng.Fori(0, PASSES) as n:
                if chain:
                    chain.enter(n, per_pass)
                for m in range(2):
                    step(2 * n + (FIRST + m), (FIRST + m) % 2)
            if chain:
                chain.leave(PASSES)
            for i in range(FIRST + 2 * PASSES, LAST + 2):
                step(i, i % 2)

        with nc.Block() as block:
            @block.sync
            def _(sp):
                def wait(name, count):
                    sp.wait_ge(s[name], count)
                    sp.sem_inc(s["sp_passed"])

                def load_x(n):
                    if later(n, 2):
                        wait("powers_ready", n - 1)
                        wait("term_ready", n - 1)
                    for half_ in range(2):
                        sp.dma_start(xc[N * half_:N * half_ + N, :, :], x[:, :, bass.ds((n - 1) * (R * C), R * C)]).then_inc(s["x_in"], 16)

                def turn_qk(n, w):
                    wait("qk_evac", n + 1)
                    if later(n, 2):
                        wait("qk_in", 16 * (n - 1))
                    sp.dma_start(scratch[w].rearrange("i g t d -> t (i g) d"),
                                 qk[:, :].rearrange("p (i d) -> p i d", d=D)).then_inc(s["qk_written"], 16)
                    wait("qk_written", 16 * (n + 1))
                    if later(n):
                        wait("qb_ready", n)
                        wait("kb_ready", n)
                    sp.dma_start(qkc[:, :, :, :].rearrange("p i b d -> p i (b d)"),
                                 scratch[w].rearrange("i g (rs b) d -> (g rs) i (b d)", b=B)).then_inc(s["qk_in"], 16)

                def store(n):
                    wait("y_ready", n + 1)
                    for r in range(R):
                        if not later(n):
                            c = slice(C // R * r, C // R * (r + 1))
                            sp.dma_start(out[c, 0, :], E[c, :]).then_inc(s["y_out"], 16)
                        else:
                            sp.dma_start(out[:, bass.ds((n - 1) * R + (1 + r), 1), :].rearrange("c o n -> c (o n)"),
                                         E[C * r:C * r + C, :]).then_inc(s["y_out"], 16)

                def start():
                    load_x(1)
                    load_x(2)
                    turn_qk(0, 0)
                    turn_qk(1, 1)

                def step(i, u):
                    attend, load, ahead = parts(i)
                    if ahead:
                        load_x(i + 2)
                    store(i - 1)
                    if load:
                        turn_qk(i + 1, 1 - u)

                steps(sp, start, step)
                sp.wait_ge(s["y_out"], 64 * GROUPS)

            @block.gpsimd
            def _(pool):
                g = nc.gpsimd
                link = Chain(pool, s["pool_chain"])
                g.tensor_copy(VB[:, :, :, G], mask_v.unsqueeze(1).to_broadcast([P, B * S, R])).then_inc(s["filled"], 1)
                at = lambda n: bass.ds((n - 1) * R, R)
                big = lambda n, col: tab[:, at(n), col:col + 8].unsqueeze(3).to_broadcast([P, R, 8, 16])
                low = lambda n, col: tab[:, at(n), col:col + 16].unsqueeze(2).to_broadcast([P, R, 8, 16])

                def term(n):
                    pool.wait_ge(s["x_in"], 32 * n)
                    if later(n, 2):
                        pool.wait_ge(s["powers_ready"], n - 1)
                    g.tensor_tensor(pt[:, :, :, :], xi.unsqueeze(2).to_broadcast([P, R, K, C]),
                                    u2[:, at(n), :].unsqueeze(3).to_broadcast([P, R, K, C]), ALU.mult).then_inc(s["term_ready"], 1)

                def powers_first(n):
                    if later(n, 2):
                        pool.wait_ge(s["tok_done"], n - 1)
                    link(g.tensor_tensor(qm[:, :, :, :], big(n, T_AR), low(n, T_B1), ALU.mult))

                def powers_second(n):
                    pool.wait_ge(s["powers_ready"], n)
                    link(g.tensor_tensor(qt, big(n, T_AI), low(n, T_B2), ALU.mult))
                    g.tensor_tensor(qm[:, :, :, :], qm[:, :, :, :], qt, ALU.add).then_inc(s["q_ready"], 1)
                    pool.wait_ge(s["q_ready"], n)

                def scale_first(n):
                    pool.wait_ge(s["var1_ready"], n + 1)
                    g.tensor_tensor(rs1, var1, half[:, :], ALU.pow).then_inc(s["rs1_ready"], 1)

                def queries(n):
                    pool.wait_ge(s["qk_in"], 16 * (n + 1))
                    if later(n):
                        pool.wait_ge(s["s_done"], n)
                    g.tensor_tensor(QA[:, :, :, :], qkc[:, 0, :, :].unsqueeze(2).to_broadcast([P, B, R, D]),
                                    mask_q.unsqueeze(1).unsqueeze(3).to_broadcast([P, B, R, D]), ALU.mult).then_inc(s["qb_ready"], 1)

                def scale_second(n, w):
                    pool.wait_ge(s["var2_ready"], n + 1)
                    link(g.tensor_tensor(rs2, var2, half[:, :], ALU.pow))
                    t = htok[w][:, :, :].rearrange("p k a -> p (k a)")
                    g.tensor_tensor(t, t, ffn_bias[:, :], ALU.add).then_inc(s["h2b_ready"], 1)

                def start():
                    term(1)
                    powers_first(1)
                    scale_first(0)
                    powers_second(1)
                    term(2)
                    powers_first(2)
                    queries(0)
                    scale_first(1)
                    for k in range(F_LO_POOL):
                        m = g.tensor_tensor(fl[:, k, :], stage[:, k, :], fh[:, k, :].bitcast(F32), ALU.subtract)
                        if k < F_LO_POOL - 1:
                            link(m)
                    m.then_inc(s["output_split_pool"], 1)
                    queries(1)
                    powers_second(2)
                    scale_second(0, 0)

                def step(i, u):
                    attend, load, ahead = parts(i)
                    if ahead:
                        term(i + 2)
                        powers_first(i + 2)
                    if load:
                        scale_first(i + 1)
                        queries(i + 1)
                    if ahead:
                        powers_second(i + 2)
                    if attend:
                        scale_second(i, u)

                steps(pool, start, step, link, 2 * 3)

            @block.scalar
            def _(act):
                a_ = nc.scalar
                link = Chain(act, s["act_chain"])

                def h_transposed(n, w):
                    if later(n):
                        act.wait_ge(s["tok_done"], n)
                        out_, src = (hw[w][:, :, :].rearrange("p k (r c) -> p r k c", r=R),
                                     T[:, :].rearrange("p (r k c) -> p r k c", r=R, k=K))
                    else:
                        out_, src = hw[w][:, :, :], clst[:, :].unsqueeze(2).to_broadcast([P, K, P])
                    if later(n, 2):
                        act.wait_ge(s["lo2_done"], n - 1)
                    a_.activation(out_, src, ACT.Copy).then_inc(s["whole_done"], 1)
                    act.wait_ge(s["whole_done"], n + 1)
                    a_.activation(hh[w][:, :, :], hw[w][:, :, :], ACT.Copy).then_inc(s["hi_done"], 1)

                def h_by_token(n, w):
                    act.wait_ge(s["trans_done"], n + 1)
                    if later(n, 2):
                        act.wait_ge(s["y_ready"], n - 1)
                    a_.activation(htok[w][:, :, :].rearrange("p k a -> p (k a)"), HT[:, :], ACT.Copy).then_inc(s["htok_ready"], 1)

                def keys(n):
                    act.wait_ge(s["qk_in"], 16 * (n + 1))
                    if later(n):
                        act.wait_ge(s["s_done"], n)
                    for q in range(S):
                        m = a_.activation(KB[:, :, q, :], qkc[:, 1, :, :], ACT.Copy, scale=mask_k[:, q:q + 1])
                        if q < S - 1:
                            link(m)
                    m.then_inc(s["kb_ready"], 1)

                def values(n):
                    act.wait_ge(s["vt_ready"], n + 1)
                    act.wait_ge(s["filled"], 1)
                    if later(n):
                        act.wait_ge(s["o_done"], n)
                    for r in range(R):
                        m = a_.activation(VB[:, :, r, 0:G], vt[:, :, :].rearrange("p g n -> p n g"), ACT.Copy, scale=mask_v[:, r:r + 1])
                        if r < R - 1:
                            link(m)
                    m.then_inc(s["vb_ready"], 1)

                def exponential(n):
                    act.wait_ge(s["sub_done"], n + 1)
                    a_.activation(E[:, :], E[:, :], ACT.Exp, scale=float(D ** -0.5)).then_inc(s["exp_done"], 1)

                def attended_hi(n, w):
                    for q, ks in enumerate(k_halves):
                        act.wait_ge(s["c_ready"], 2 * n + (q + 1))
                        a_.activation(hh[w][:, ks, :], hw[w][:, ks, :], ACT.Copy).then_inc(s["hi2_done"], 1)

                def start():
                    h_transposed(0, 0)
                    a_.activation(fh[:, K - 1, :], stage[:, K - 1, :], ACT.Copy).then_inc(s["last_hi"], 1)
                    h_by_token(0, 0)
                    h_transposed(1, 1)
                    h_by_token(1, 1)
                    keys(0)
                    values(0)
                    exponential(0)
                    attended_hi(0, 0)
                    keys(1)
                    values(1)

                def step(i, u):
                    attend, load, ahead = parts(i)
                    if attend:
                        exponential(i)
                    if load:
                        h_transposed(i + 1, 1 - u)
                        h_by_token(i + 1, 1 - u)
                    if attend:
                        attended_hi(i, u)
                    if load:
                        keys(i + 1)
                        values(i + 1)

                steps(act, start, step, link, 2 * 6)

            @block.tensor
            def _(pe):
                mm = nc.tensor.matmul

                def passes(dst, w, hi, lo, cols):
                    of = [(hh[w], k, a) for k in range(K) for a in (hi, lo)] + [(hl[w], k, hi) for k in range(K)]
                    return [lambda n=n, t=t, k=k, a=a: mm(dst, t[:, k, :], a[:, k, cols], start=(n == 0), stop=(n == 3 * K - 1))
                            for n, (t, k, a) in enumerate(of)]

                def run(group):
                    for one in group:
                        m = one()
                    return m

                def h_transposed(n, scored):
                    pe.wait_ge(s["powers_ready"], n)
                    pe.wait_ge(s["q_ready"], n)
                    if scored:
                        pe.wait_ge(s["sub_done"], n)
                    for r in range(R):
                        m = mm(T[:, 256 * r:256 * r + 256], qm[:, r, :, :].rearrange("p a b -> p (a b)"),
                               pm[:, r, :, :].rearrange("p k c -> p (k c)"), start=True, stop=True)
                    m.then_inc(s["tok_done"], 1)

                def h_by_token(n, w):
                    pe.wait_ge(s["whole_done"], n + 1)
                    if later(n):
                        pe.wait_ge(s["htok_ready"], n)
                    for k in range(K):
                        m = nc.tensor.transpose(HT[:, P * k:P * k + P], hw[w][:, k, :], ident)
                    m.then_inc(s["trans_done"], 1)

                queries_keys = lambda w: passes(Q[:, 0:QK], w, wh, wl, slice(0, QK))

                def queries_keys_hi(n, w):
                    pe.wait_ge(s["hi_done"], n + 1)
                    if later(n):
                        pe.wait_ge(s["qk_evac"], n)
                    run(queries_keys(w)[:2 * K])

                def queries_keys_lo(n, w):
                    pe.wait_ge(s["lo_done"], n + 1)
                    run(queries_keys(w)[2 * K:]).then_inc(s["qk_done"], 1)

                value_passes = lambda w: passes(Q[:, QK:QKV], w, wh, wl, slice(QK, QKV))

                def values_first(n, w):
                    if later(n):
                        pe.wait_ge(s["vt_ready"], n)
                    run(value_passes(w)[:V_FIRST])

                def values_second(w):
                    run(value_passes(w)[V_FIRST:]).then_inc(s["v_done"], 1)

                def scores(n):
                    pe.wait_ge(s["qb_ready"], n + 1)
                    pe.wait_ge(s["kb_ready"], n + 1)
                    for b in range(B):
                        m = mm(T[:, P * b:P * b + P], QA[:, b, :, :].rearrange("p r d -> p (r d)"),
                               KB[:, b, :, :].rearrange("p s e -> p (s e)"), start=True, stop=True)
                    m.then_inc(s["s_done"], 1)

                def attention(n):
                    pe.wait_ge(s["et_ready"], n + 1)
                    pe.wait_ge(s["vb_ready"], n + 1)
                    if later(n):
                        pe.wait_ge(s["y0_done"], n)
                    for i in range(B * S):
                        b, q = i // S, i % S
                        m = mm(O[32 * q:32 * q + 32, b, :, :].rearrange("p r g -> p (r g)"),
                               ET[:, i, :], VB[:, B * q + b, :, :].rearrange("p r g -> p (r g)"), start=True, stop=True)
                    m.then_inc(s["o_done"], 1)

                def attention_turned(n):
                    pe.wait_ge(s["ot_ready"], n + 1)
                    if later(n):
                        pe.wait_ge(s["y_ready"], n)
                    for q in range(2):
                        m = nc.tensor.transpose(OT[:, q, :], ot[:, P * q:P * q + P], ident)
                    m.then_inc(s["ott_done"], 1)
                    mm(OTOK[:, :], perm, ot[:, :], start=True, stop=True).then_inc(s["otok_done"], 1)

                second_half = lambda w: passes(F[:, 512:1024], w, fh, fl, slice(512, 1024))

                def output_first(n, w):
                    first_half = passes(F[:, 0:512], w, fh, fl, slice(0, 512))
                    for q in range(2):
                        pe.wait_ge(s["hi2_done"], 2 * n + (q + 1))
                        run(first_half[K * q:K * q + K])
                    pe.wait_ge(s["lo2_done"], n + 1)
                    run(first_half[2 * K:]).then_inc(s["f0_done"], 1)
                    pe.wait_ge(s["otok_read"], n + 1)
                    run(second_half(w)[:F1_FIRST])

                def start():
                    h_by_token(0, 0)
                    pe.wait_ge(s["queries_split"], 1)
                    queries_keys_hi(0, 0)
                    queries_keys_lo(0, 0)
                    values_first(0, 0)
                    values_second(0)
                    h_transposed(1, scored=False)
                    h_by_token(1, 1)
                    queries_keys_hi(1, 1)
                    scores(0)
                    queries_keys_lo(1, 1)
                    values_first(1, 1)
                    attention(0)
                    attention_turned(0)
                    values_second(1)
                    pe.wait_ge(s["output_split"], K - F_LO_POOL)
                    pe.wait_ge(s["output_split_pool"], 1)

                def step(i, u):
                    attend, load, ahead = parts(i)
                    output_first(i - 1, 1 - u)
                    if attend:
                        scores(i)
                    run(second_half(1 - u)[F1_FIRST:F1_SECOND])
                    if load:
                        h_transposed(i + 1, scored=True)
                    run(second_half(1 - u)[F1_SECOND:]).then_inc(s["f1_done"], 1)
                    if load:
                        h_by_token(i + 1, 1 - u)
                        queries_keys_hi(i + 1, 1 - u)
                        queries_keys_lo(i + 1, 1 - u)
                    if attend:
                        attention(i)
                    if load:
                        values_first(i + 1, 1 - u)
                    if attend:
                        attention_turned(i)
                    if load:
                        values_second(1 - u)

                steps(pe, start, step)

            @block.vector
            def _(dve):
                v = nc.vector
                link = Chain(dve, s["dve_chain"])
                tt = lambda o, a, b, op: link(v.tensor_tensor(o, a, b, op))

                def signal(ins, name, count):
                    ins.then_inc(s[name], 1)
                    dve.wait_ge(s[name], count)

                def variance(t, stats, mv, var, name, count):
                    for i in range(2):
                        link(v.bn_stats(stats[:, 6 * i:6 * i + 6], t[:, 4 * i:4 * i + 4, :].rearrange("p k a -> p (k a)")))
                    dve.sem_inc(s["dve_passed"])
                    link(v.bn_aggr(mv[:, :], stats))
                    signal(v.tensor_scalar(var, mv[:, 1:2], EPS, None, ALU.add), name, count)

                def powers_first(n):
                    dve.wait_ge(s["x_in"], 32 * n)
                    if later(n, 2):
                        dve.wait_ge(s["tok_done"], n - 1)
                    tt(pm[:, :, :, :], xr.unsqueeze(2).to_broadcast([P, R, K, C]),
                       u1[:, bass.ds((n - 1) * R, R), :].unsqueeze(3).to_broadcast([P, R, K, C]), ALU.mult)

                def powers_second(n):
                    dve.wait_ge(s["term_ready"], n)
                    signal(v.tensor_tensor(pm[:, :, :, :], pm[:, :, :, :], pt[:, :, :, :], ALU.add), "powers_ready", n)

                def h_lo(n, w):
                    dve.wait_ge(s["hi_done"], n + 1)
                    if later(n, 2):
                        dve.wait_ge(s["f1_done"], n - 1)
                    signal(v.tensor_tensor(hl[w][:, :, :], hw[w][:, :, :], hh[w][:, :, :].bitcast(F32), ALU.subtract), "lo_done", n + 1)

                def variance_first(n, w):
                    dve.wait_ge(s["htok_ready"], n + 1)
                    if later(n):
                        dve.wait_ge(s["rs1_ready"], n)
                    variance(htok[w], bn[:, 0, :], mv1, var1, "var1_ready", n + 1)

                def queries_keys(n):
                    dve.wait_ge(s["rs1_ready"], n + 1)
                    dve.wait_ge(s["qk_done"], n + 1)
                    if later(n):
                        dve.wait_ge(s["qk_written"], 16 * n)
                    signal(v.scalar_tensor_tensor(qk[:, :], Q[:, 0:QK], rs1, qkv_bias[:, 0:QK], ALU.mult, ALU.add), "qk_evac", n + 1)

                def values(n):
                    dve.wait_ge(s["v_done"], n + 1)
                    link(v.scalar_tensor_tensor(vs, Q[:, QK:QKV], rs1, qkv_bias[:, QK:QKV], ALU.mult, ALU.add))
                    if later(n):
                        dve.wait_ge(s["vb_ready"], n)
                    signal(v.transpose(vt[:, :, :].rearrange("p g n -> p (g n)"), vs), "vt_ready", n + 1)

                def scores(n):
                    dve.wait_ge(s["s_done"], n + 1)
                    sc = T[:, :].rearrange("p (n e) -> p n e", e=D)
                    link(v.tensor_reduce(mx[:, :], sc, AX_X, ALU.max))
                    signal(v.tensor_tensor(E[:, :].rearrange("p (n e) -> p n e", e=D), sc,
                                           mx[:, :].unsqueeze(2).to_broadcast([P, B * S, D]), ALU.subtract), "sub_done", n + 1)

                def weights(n):
                    dve.wait_ge(s["exp_done"], n + 1)
                    signal(v.transpose(ET[:, :, :].rearrange("p n d -> p (n d)"), E[:, :]), "et_ready", n + 1)

                def attention(n):
                    dve.wait_ge(s["o_done"], n + 1)
                    link(v.reciprocal(rden[:, :].rearrange("p (b r) -> p b r", b=B), O[:, :, :, G]))
                    flat = F[:, 0:B * R * GV].rearrange("p (n g) -> p g n", g=GV)[:, 0:G, :]
                    tt(on[:, :, :], flat, rden[:, :].unsqueeze(1).to_broadcast([P, G, 32]), ALU.mult)
                    if later(n):
                        dve.wait_ge(s["otok_done"], n)
                    signal(v.transpose(ot[:, :].rearrange("p (q d gh) -> p gh q d", q=2, gh=4),
                                       on[:, :, :].rearrange("p (gh q) n -> p gh q n", q=2)), "ot_ready", n + 1)

                def attended(n, w):
                    dve.wait_ge(s["ott_done"], n + 1)
                    for q, ks in enumerate(k_halves):
                        c = hw[w][:, ks, :].rearrange("p m (r c) -> p m r c", r=R)
                        by_token = OT[:, q, :].rearrange("p (c r) -> p r c", r=R).unsqueeze(1).to_broadcast([P, J, R, C])
                        signal(v.tensor_tensor(c, c, by_token, ALU.add), "c_ready", 2 * n + (q + 1))
                    dve.wait_ge(s["otok_done"], n + 1)
                    c = htok[w][:, :, :].rearrange("p (q m) a -> p q m a", q=2)
                    signal(v.tensor_tensor(c, c, OTOK.rearrange("p (q a) -> p q a", q=2).unsqueeze(2).to_broadcast([P, 2, J, P]),
                                           ALU.add), "otok_read", n + 1)
                    dve.wait_ge(s["hi2_done"], 2 * n + 2)
                    signal(v.tensor_tensor(hl[w][:, :, :], hw[w][:, :, :], hh[w][:, :, :].bitcast(F32), ALU.subtract), "lo2_done", n + 1)

                def variance_second(n, w):
                    if later(n):
                        dve.wait_ge(s["h2b_ready"], n)
                    variance(htok[w], bn[:, 1, :], mv2, var2, "var2_ready", n + 1)

                def rows(n, w):
                    dve.wait_ge(s["h2b_ready"], n + 1)
                    for half_, (done, name) in enumerate((("f0_done", "y0_done"), ("f1_done", "y_ready"))):
                        at = slice(512 * half_, 512 * half_ + 512)
                        dve.wait_ge(s[done], n + 1)
                        signal(v.scalar_tensor_tensor(
                            E[:, at].rearrange("p (a k) -> p a k", k=K), F[:, at].rearrange("p (a k) -> p a k", k=K), rs2,
                            htok[w][:, :, 64 * half_:64 * half_ + 64].rearrange("p k a -> p a k"), ALU.mult, ALU.add), name, n + 1)

                def output_lo(first, end):
                    for k in range(first, end):
                        if k == K - 1:
                            dve.wait_ge(s["last_hi"], 1)
                        signal(v.tensor_tensor(fl[:, k, :], stage[:, k, :], fh[:, k, :].bitcast(F32), ALU.subtract),
                               "output_split", k - F_LO_POOL + 1)

                def start():
                    at = slice(0, G * D)
                    signal(v.tensor_tensor(wl[:, :, at], wsum[:, :, at], wh[:, :, at].bitcast(F32), ALU.subtract), "queries_split", 1)
                    h_lo(0, 0)
                    variance_first(0, 0)
                    powers_first(1)
                    powers_second(1)
                    queries_keys(0)
                    output_lo(F_LO_POOL, F_LO_POOL + 1)
                    values(0)
                    output_lo(F_LO_POOL + 1, K - 1)
                    h_lo(1, 1)
                    variance_first(1, 1)
                    output_lo(K - 1, K)
                    scores(0)
                    queries_keys(1)
                    weights(0)
                    attention(0)
                    attended(0, 0)
                    powers_first(2)
                    powers_second(2)
                    values(1)
                    variance_second(0, 0)

                def step(i, u):
                    attend, load, ahead = parts(i)
                    if later(i, 2):
                        dve.wait_ge(s["y_out"], 64 * (i - 1))
                    if attend:
                        scores(i)
                        weights(i)
                    rows(i - 1, 1 - u)
                    if load:
                        h_lo(i + 1, 1 - u)
                    if load:
                        variance_first(i + 1, 1 - u)
                    if ahead:
                        powers_first(i + 2)
                    if load:
                        queries_keys(i + 1)
                    if attend:
                        attention(i)
                    if attend:
                        attended(i, u)
                    if ahead:
                        powers_second(i + 2)
                    if load:
                        values(i + 1)
                    if attend:
                        variance_second(i, u)

                steps(dve, start, step, link, 2 * 11)


def kernel(x, cls_tok, L0_tok_A_abslog, L0_tok_A_phase, L0_attn_Wq, L0_attn_bq, L0_attn_Wk, L0_attn_bk,
           L0_attn_Wv, L0_attn_bv, L0_ffn_W, L0_ffn_bias, L0_ffn_A, L0_ffn_Bf, L0_ffn_coeffs, L0_ffn_scales):
    import concourse.bacc as bacc
    from concourse.bass_utils import run_bass_kernel_spmd

    def by_group(w):
        w = np.asarray(w)
        w = w.reshape(*w.shape[:-1], G, w.shape[-1] // G)
        w = np.moveaxis(w, -2, -3)
        return w.reshape(*w.shape[:-3], -1)

    chunked = lambda w: np.moveaxis(w.reshape(*w.shape[:-1], P, K), -1, -2).reshape(*w.shape[:-1], L)
    arrays = {
        "x": np.ascontiguousarray(np.transpose(np.asarray(x), (2, 3, 1, 0)).reshape(N, 2, H * C)),
        "modes": np.stack([np.asarray(L0_tok_A_phase).T, np.asarray(L0_tok_A_abslog).T], 1),
        "cls": np.ascontiguousarray(np.asarray(cls_tok).reshape(L)),
        "wq": np.ascontiguousarray(by_group(L0_attn_Wq)),
        "wkv": np.ascontiguousarray(np.concatenate([by_group(L0_attn_Wk), by_group(L0_attn_Wv)], -1)),
        "bq": np.ascontiguousarray(by_group(L0_attn_bq)),
        "bkv": np.ascontiguousarray(np.concatenate([by_group(L0_attn_bk), by_group(L0_attn_bv)], -1)),
        "wt": np.ascontiguousarray(np.asarray(L0_ffn_W).T),
        "fbias": np.ascontiguousarray(chunked(np.asarray(L0_ffn_bias))),
        "fa": np.ascontiguousarray(chunked(np.asarray(L0_ffn_A).reshape(ER, L))),
        "fb": np.ascontiguousarray(np.transpose(np.asarray(L0_ffn_Bf), (0, 2, 1)).reshape(ER, L)),
        "gates": np.ascontiguousarray(np.concatenate([np.repeat(np.asarray(a), 16).reshape(2, P)
                                       for a in (L0_ffn_coeffs, L0_ffn_scales)]).T),
        "const": constants(),
        "maps": part_maps(),
    }
    nc = bacc.Bacc("TRN2", target_bir_lowering=False, num_devices=1)
    ins = [nc.dram_tensor(f"in_{n}", a.shape, mybir.dt.from_np(a.dtype), kind="ExternalInput").ap()
           for n, a in arrays.items()]
    y = nc.dram_tensor("out_rows", (C, H + 1, L), F32, kind="ExternalOutput").ap()
    tower(nc, *ins, y)
    r = run_bass_kernel_spmd(nc, [{f"in_{n}": a for n, a in arrays.items()}], core_ids=[0])
    return r.results[0]["out_rows"]
```
